# Optimizing a Trainium2 kernel written in Bass

```python
import numpy as np
import jax
import jax.numpy as jnp

def _softmax(x, axis=-1):
    return jax.nn.softmax(x, axis=axis)

def _gelu(x):
    return jax.nn.gelu(x, approximate=True)

def _silu(x):
    return jax.nn.silu(x)

def _sigmoid(x):
    return jax.nn.sigmoid(x)

def _layernorm(x, axis=-1, eps=1e-05):
    m = jnp.mean(x, axis=axis, keepdims=True)
    v = jnp.var(x, axis=axis, keepdims=True)
    return (x - m) / jnp.sqrt(v + eps)

def _scatter_add(tgt, idx, src, axis=0):
    return tgt.at[idx].add(src)

def _segment_sum(src, seg, n):
    return jax.ops.segment_sum(src, seg, n)
kernel_name = 'mk_macaron_d1_jaxref_r4_378460'

def setup_inputs(seed: int=0):
    np.random.seed(seed)
    _w = jnp.asarray

    def _L0_attn_setup():
        import math
        import jax, jax.numpy as jnp
        import numpy as np
        N_EMBD = 256
        N_HEAD = 16
        NUM_BUCKETS = 32
        MAX_DISTANCE = 128

        def _relative_position_bucket(relative_position, num_buckets=NUM_BUCKETS, max_distance=MAX_DISTANCE):
            rp = -jnp.minimum(relative_position, 0)
            max_exact = num_buckets // 2
            is_small = rp < max_exact
            rp_large = max_exact + (jnp.log(rp.astype(jnp.float32) / max_exact + 1e-10) / math.log(max_distance / max_exact) * (num_buckets - max_exact)).astype(jnp.int32)
            rp_large = jnp.minimum(rp_large, num_buckets - 1)
            return jnp.where(is_small, rp, rp_large)
        key = jax.random.key(seed)
        ks = jax.random.split(key, 6)
        B, T, C = (4, 512, N_EMBD)
        s_in = 1.0 / math.sqrt(C)
        x = jax.random.normal(ks[0], (B, T, C), dtype=jnp.float32)
        W_attn = jax.random.normal(ks[1], (3 * C, C), dtype=jnp.float32) * s_in
        b_attn = jnp.zeros((3 * C,), dtype=jnp.float32)
        W_proj = jax.random.normal(ks[2], (C, C), dtype=jnp.float32) * s_in
        b_proj = jnp.zeros((C,), dtype=jnp.float32)
        rel_emb = jax.random.normal(ks[3], (NUM_BUCKETS, N_HEAD), dtype=jnp.float32) * 0.02
        return {'x': x, 'W_attn': W_attn, 'b_attn': b_attn, 'W_proj': W_proj, 'b_proj': b_proj, 'rel_emb': rel_emb}
    _L0_attn_in = _L0_attn_setup()

    def _L0_ffn_setup():
        import jax, jax.numpy as jnp
        import numpy as np
        D = 256
        H = 4
        HD = D // H
        E = 8
        FF = 1024
        CAP_FACTOR = 1.0

        def _ln(x, g, b, eps=1e-05):
            mu = jnp.mean(x, -1, keepdims=True)
            v = jnp.mean((x - mu) ** 2, -1, keepdims=True)
            return (x - mu) * jax.lax.rsqrt(v + eps) * g + b

        def _mha(x, w, b, ow, ob):
            L, N, _ = x.shape
            qkv = x @ w.T + b
            q, k, v = jnp.split(qkv, 3, axis=-1)
            rh = lambda t: t.reshape(L, N, H, HD).transpose(1, 2, 0, 3)
            q, k, v = (rh(q), rh(k), rh(v))
            scores = jnp.einsum('nhld,nhmd->nhlm', q, k) / np.float32(np.sqrt(HD))
            attn = jax.nn.softmax(scores, axis=-1)
            o = jnp.einsum('nhlm,nhmd->nhld', attn, v).transpose(2, 0, 1, 3).reshape(L, N, D)
            return o @ ow.T + ob

        def _moe(x, wg, w1, b1, w2, b2):
            L, N, _ = x.shape
            S = L * N
            cap = int(CAP_FACTOR * S) // E
            xf = x.reshape(S, D)
            gates = jax.nn.softmax(xf @ wg, axis=-1)
            idx = jnp.argmax(gates, axis=-1)
            mask1 = jax.nn.one_hot(idx, E, dtype=x.dtype)
            loc = jnp.sum((jnp.cumsum(mask1, 0) - 1.0) * mask1, -1).astype(jnp.int32)
            keep = loc < cap
            gate_val = jnp.take_along_axis(gates, idx[:, None], -1)[:, 0]
            slot = jnp.where(keep, idx.astype(jnp.int32) * cap + loc, E * cap)
            disp = jnp.zeros((E * cap, D), x.dtype).at[slot].set(xf, mode='drop')
            disp = disp.reshape(E, cap, D)
            h = jnp.einsum('ecd,edf->ecf', disp, w1) + b1[:, None, :]
            y = (jnp.einsum('ecf,efd->ecd', h, w2) + b2[:, None, :]).reshape(E * cap, D)
            out = jnp.where(keep[:, None], gate_val[:, None] * y[jnp.minimum(slot, E * cap - 1)], 0.0)
            return out.reshape(L, N, D)
        key = jax.random.key(seed)
        ks = jax.random.split(key, 8)
        L, N = (256, 16)
        s = 0.02
        return {'x': jax.random.normal(ks[0], (L, N, D), jnp.float32), 'in_proj_w': jax.random.normal(ks[1], (3 * D, D), jnp.float32) * s, 'in_proj_b': jnp.zeros((3 * D,), jnp.float32), 'out_proj_w': jax.random.normal(ks[2], (D, D), jnp.float32) * s, 'out_proj_b': jnp.zeros((D,), jnp.float32), 'ln1_g': jnp.ones((D,), jnp.float32), 'ln1_b': jnp.zeros((D,), jnp.float32), 'ln2_g': jnp.ones((D,), jnp.float32), 'ln2_b': jnp.zeros((D,), jnp.float32), 'wg': jax.random.normal(ks[3], (D, E), jnp.float32) * s, 'w1': jax.random.normal(ks[4], (E, D, FF), jnp.float32) * s, 'b1': jnp.zeros((E, FF), jnp.float32), 'w2': jax.random.normal(ks[5], (E, FF, D), jnp.float32) * s, 'b2': jnp.zeros((E, D), jnp.float32)}
    _L0_ffn_in = _L0_ffn_setup()
    _d = {'L0_attn_x': _L0_attn_in['x'], 'L0_attn_W_attn': _L0_attn_in['W_attn'], 'L0_attn_b_attn': _L0_attn_in['b_attn'], 'L0_attn_W_proj': _L0_attn_in['W_proj'], 'L0_attn_b_proj': _L0_attn_in['b_proj'], 'L0_attn_rel_emb': _L0_attn_in['rel_emb'], 'L0_ffn_in_proj_w': _L0_ffn_in['in_proj_w'], 'L0_ffn_in_proj_b': _L0_ffn_in['in_proj_b'], 'L0_ffn_out_proj_w': _L0_ffn_in['out_proj_w'], 'L0_ffn_out_proj_b': _L0_ffn_in['out_proj_b'], 'L0_ffn_ln1_g': _L0_ffn_in['ln1_g'], 'L0_ffn_ln1_b': _L0_ffn_in['ln1_b'], 'L0_ffn_ln2_g': _L0_ffn_in['ln2_g'], 'L0_ffn_ln2_b': _L0_ffn_in['ln2_b'], 'L0_ffn_wg': _L0_ffn_in['wg'], 'L0_ffn_w1': _L0_ffn_in['w1'], 'L0_ffn_b1': _L0_ffn_in['b1'], 'L0_ffn_w2': _L0_ffn_in['w2'], 'L0_ffn_b2': _L0_ffn_in['b2']}
    _x0 = _d['L0_attn_x']
    _d['L0_attn_x'] = jax.random.normal(jax.random.fold_in(jax.random.key(seed), 1), (8, 1024, 256), dtype=_x0.dtype)
    del _x0
    return _d

def reference(L0_attn_x, L0_attn_W_attn, L0_attn_b_attn, L0_attn_W_proj, L0_attn_b_proj, L0_attn_rel_emb, L0_ffn_in_proj_w, L0_ffn_in_proj_b, L0_ffn_out_proj_w, L0_ffn_out_proj_b, L0_ffn_ln1_g, L0_ffn_ln1_b, L0_ffn_ln2_g, L0_ffn_ln2_b, L0_ffn_wg, L0_ffn_w1, L0_ffn_b1, L0_ffn_w2, L0_ffn_b2):

    def _L0_attn_ref(x, W_attn, b_attn, W_proj, b_proj, rel_emb):
        import math
        import jax, jax.numpy as jnp
        import numpy as np
        N_EMBD = 256
        N_HEAD = 16
        NUM_BUCKETS = 32
        MAX_DISTANCE = 128

        def _relative_position_bucket(relative_position, num_buckets=NUM_BUCKETS, max_distance=MAX_DISTANCE):
            rp = -jnp.minimum(relative_position, 0)
            max_exact = num_buckets // 2
            is_small = rp < max_exact
            rp_large = max_exact + (jnp.log(rp.astype(jnp.float32) / max_exact + 1e-10) / math.log(max_distance / max_exact) * (num_buckets - max_exact)).astype(jnp.int32)
            rp_large = jnp.minimum(rp_large, num_buckets - 1)
            return jnp.where(is_small, rp, rp_large)
        B, T, C = x.shape
        H = N_HEAD
        D = C // H
        qkv = x @ W_attn.T + b_attn
        q, k, v = jnp.split(qkv, 3, axis=-1)
        q = q.reshape(B, T, H, D).transpose(0, 2, 1, 3)
        k = k.reshape(B, T, H, D).transpose(0, 2, 1, 3)
        v = v.reshape(B, T, H, D).transpose(0, 2, 1, 3)
        pos = jnp.arange(T)
        rel_pos = pos[None, :] - pos[:, None]
        buckets = _relative_position_bucket(rel_pos)
        rel_bias = rel_emb[buckets]
        rel_bias = rel_bias.transpose(2, 0, 1)[None]
        att = jnp.einsum('bhqd,bhkd->bhqk', q, k) * (1.0 / math.sqrt(D))
        att = att + rel_bias
        causal = jnp.tril(jnp.ones((T, T), dtype=bool))
        att = jnp.where(causal[None, None], att, -jnp.inf)
        att = jax.nn.softmax(att, axis=-1)
        y = jnp.einsum('bhqk,bhkd->bhqd', att, v)
        y = y.transpose(0, 2, 1, 3).reshape(B, T, C)
        y = y @ W_proj.T + b_proj
        return y

    def _L0_ffn_ref(x, in_proj_w, in_proj_b, out_proj_w, out_proj_b, ln1_g, ln1_b, ln2_g, ln2_b, wg, w1, b1, w2, b2):
        import jax, jax.numpy as jnp
        import numpy as np
        D = 256
        H = 4
        HD = D // H
        E = 8
        FF = 1024
        CAP_FACTOR = 1.0

        def _ln(x, g, b, eps=1e-05):
            mu = jnp.mean(x, -1, keepdims=True)
            v = jnp.mean((x - mu) ** 2, -1, keepdims=True)
            return (x - mu) * jax.lax.rsqrt(v + eps) * g + b

        def _mha(x, w, b, ow, ob):
            L, N, _ = x.shape
            qkv = x @ w.T + b
            q, k, v = jnp.split(qkv, 3, axis=-1)
            rh = lambda t: t.reshape(L, N, H, HD).transpose(1, 2, 0, 3)
            q, k, v = (rh(q), rh(k), rh(v))
            scores = jnp.einsum('nhld,nhmd->nhlm', q, k) / np.float32(np.sqrt(HD))
            attn = jax.nn.softmax(scores, axis=-1)
            o = jnp.einsum('nhlm,nhmd->nhld', attn, v).transpose(2, 0, 1, 3).reshape(L, N, D)
            return o @ ow.T + ob

        def _moe(x, wg, w1, b1, w2, b2):
            L, N, _ = x.shape
            S = L * N
            cap = int(CAP_FACTOR * S) // E
            xf = x.reshape(S, D)
            gates = jax.nn.softmax(xf @ wg, axis=-1)
            idx = jnp.argmax(gates, axis=-1)
            mask1 = jax.nn.one_hot(idx, E, dtype=x.dtype)
            loc = jnp.sum((jnp.cumsum(mask1, 0) - 1.0) * mask1, -1).astype(jnp.int32)
            keep = loc < cap
            gate_val = jnp.take_along_axis(gates, idx[:, None], -1)[:, 0]
            slot = jnp.where(keep, idx.astype(jnp.int32) * cap + loc, E * cap)
            disp = jnp.zeros((E * cap, D), x.dtype).at[slot].set(xf, mode='drop')
            disp = disp.reshape(E, cap, D)
            h = jnp.einsum('ecd,edf->ecf', disp, w1) + b1[:, None, :]
            y = (jnp.einsum('ecf,efd->ecd', h, w2) + b2[:, None, :]).reshape(E * cap, D)
            out = jnp.where(keep[:, None], gate_val[:, None] * y[jnp.minimum(slot, E * cap - 1)], 0.0)
            return out.reshape(L, N, D)
        y1 = _ln(x + _mha(x, in_proj_w, in_proj_b, out_proj_w, out_proj_b), ln1_g, ln1_b)
        y2 = _ln(y1 + _moe(y1, wg, w1, b1, w2, b2), ln2_g, ln2_b)
        return y2
    x = L0_attn_x
    x = x + 0.5 * _L0_ffn_ref(_layernorm(x, axis=-1), L0_ffn_in_proj_w, L0_ffn_in_proj_b, L0_ffn_out_proj_w, L0_ffn_out_proj_b, L0_ffn_ln1_g, L0_ffn_ln1_b, L0_ffn_ln2_g, L0_ffn_ln2_b, L0_ffn_wg, L0_ffn_w1, L0_ffn_b1, L0_ffn_w2, L0_ffn_b2)
    x = x + _L0_attn_ref(_layernorm(x, axis=-1), L0_attn_W_attn, L0_attn_b_attn, L0_attn_W_proj, L0_attn_b_proj, L0_attn_rel_emb)
    x = x + 0.5 * _L0_ffn_ref(_layernorm(x, axis=-1), L0_ffn_in_proj_w, L0_ffn_in_proj_b, L0_ffn_out_proj_w, L0_ffn_out_proj_b, L0_ffn_ln1_g, L0_ffn_ln1_b, L0_ffn_ln2_g, L0_ffn_ln2_b, L0_ffn_wg, L0_ffn_w1, L0_ffn_b1, L0_ffn_w2, L0_ffn_b2)
    return x

_drawn_inputs = setup_inputs


def setup_inputs(seed=0):
    import zlib

    import numpy as np

    out = dict(_drawn_inputs(seed))
    spreads = {'L0_attn_b_attn': (0.0, 0.1),
     'L0_attn_b_proj': (0.0, 0.1),
     'L0_ffn_in_proj_b': (0.0, 0.394),
     'L0_ffn_out_proj_b': (0.0, 0.1),
     'L0_ffn_ln1_g': (1.0, 0.2),
     'L0_ffn_ln1_b': (0.0, 0.1),
     'L0_ffn_ln2_g': (1.0, 0.2),
     'L0_ffn_ln2_b': (0.0, 0.1),
     'L0_ffn_b1': (0.0, 0.8),
     'L0_ffn_b2': (0.0, 0.798)}
    factors = {'L0_attn_rel_emb': 44.127, 'L0_ffn_w1': 2.704}
    for name, (base, spread) in spreads.items():
        noise = np.random.default_rng([zlib.crc32(name.encode()), seed]).standard_normal(out[name].shape)
        drawn = base * np.exp(spread * noise) if base else spread * noise
        out[name] = jnp.asarray(drawn.astype(out[name].dtype))
    for name, factor in factors.items():
        out[name] = (out[name] * factor).astype(out[name].dtype)
    return out
```

```python
from contextlib import ExitStack

import numpy as np

import concourse.bass as bass
from concourse import mybir

F32 = mybir.dt.float32
BF16 = mybir.dt.bfloat16
I32 = mybir.dt.int32
U32 = mybir.dt.uint32
ALU = mybir.AluOpType
ACT = mybir.ActivationFunctionType
AX = mybir.AxisListType

P = 128
B, T, C = 8, 1024, 256
S = B * T
KB = C // P
TILES = S // P
GT = 4
GW = GT * P
NG = TILES // GT
EPS = 1e-5
FH = 4
FD = C // FH
NE = 8
FF = 1024
CAP = S // NE
AH = 16
AD = C // AH
HG = 4
NHG = AH // HG
QB = T // P
NBUCKET, MAXDIST = 32, 128
BIG = 1e30


def bucket_starts():
    half = NBUCKET // 2
    d = np.arange(2 * P)
    far = half + (np.log(np.maximum(d, half).astype(np.float32) / np.float32(half) + np.float32(1e-10))
                  / np.float32(np.log(MAXDIST / half)) * np.float32(NBUCKET - half)).astype(np.int32)
    bucket = np.where(d < half, d, np.minimum(far, NBUCKET - 1))
    return [int(np.argmax(bucket == b)) if (bucket == b).any() else None for b in range(NBUCKET)]


class Core:

    def __init__(self, nc, ctx):
        self.nc, self.ctx = nc, ctx
        self.ps = ctx.enter_context(nc.psum_tensor("banks", [P, 8, 512], F32))
        self.indirect = [ctx.enter_context(nc.semaphore(f"indirect{i}")) for i in range(8)]

    def keep(self, name, shape, dt=F32):
        return self.ctx.enter_context(self.nc.sbuf_tensor(name, shape, dt))


class Phase(ExitStack):

    def __init__(self, core, name):
        super().__init__()
        self.core, self.name, self.sems = core, name, []

    def sb(self, name, shape, dt=F32):
        return self.enter_context(self.core.nc.sbuf_tensor(f"{self.name}_{name}", shape, dt))

    def sem(self, name):
        sem = self.enter_context(self.core.nc.semaphore(f"{self.name}_{name}"))
        self.sems.append(sem)
        return sem

    def block(self):
        self.callback(self._clear)
        return self.enter_context(self.core.nc.Block())

    def _clear(self):
        for sem in self.sems:
            self.core.nc.gpsimd.sem_clear(sem)
        self.core.nc.all_engine_barrier()


def wait_apart(eng, sem, value):
    eng.wait_ge(sem, value)
    if not isinstance(value, int):
        eng.nop(nofuse=True)


def row_bcast(ap_1d, n):
    return bass.AP(tensor=ap_1d.tensor, offset=ap_1d.offset, ap=[[0, P], [1, n]])


def groups(eng, count, lo, hi, body):
    for g in range(lo):
        body(g, g % 2)
    with eng.Fori(lo // 2, (count - hi) // 2) as it:
        for u in range(2):
            body(it * 2 + u, u)
    for g in range(count - hi, count):
        body(g, g % 2)


def under(g, k):
    return isinstance(g, int) and g < k


def over(ap, count, at):
    return ap.unsqueeze(at).to_broadcast(list(ap.shape[:at]) + [count] + list(ap.shape[at:]))



def prepare_constants(core, d, relrow, neard):
    nc = core.nc
    core.ident = core.keep("ident", [P, P])
    core.identb = core.keep("identb", [P, P], BF16)
    core.mask = core.keep("mask", [P, 4 * P], BF16)
    core.before = core.keep("before", [P, P])
    core.ones = core.keep("ones", [P, P])
    core.winT = core.keep("winT", [P, KB, 3 * C])
    core.woutT = core.keep("woutT", [P, KB, C])
    core.wattnT = core.keep("wattnT", [P, KB, 3 * C])
    core.wprojT = core.keep("wprojT", [P, KB, C])
    core.wg = core.keep("wg", [P, KB, NE])
    core.rows = {k: core.keep("row_" + k, [P, C]) for k in
                 ("ffn_v", "ffn_out", "ln1_g", "ln1_b", "ln2_g", "ln2_b", "attn_v", "proj")}
    core.ffn_qk_b = core.keep("ffn_qk_b", [P, 4])
    core.attn_qk_b = core.keep("attn_qk_b", [P, 4])
    core.mhalf = core.keep("mhalf", [P, GT])
    starts = bucket_starts()
    order = [(b, s) for b, s in enumerate(starts) if s is not None]
    with Phase(core, "const") as ph:
        wraw = ph.sb("wraw", [P, 16, C])
        hankel = ph.sb("hankel", [P, AH, 2 * P])
        toeplitz = ph.sb("toeplitz", [P, AH, 2 * P])
        flip = ph.sb("flip", [P, P])
        embT = ph.sb("embT", [AH, NBUCKET])
        rel = ph.sb("rel", [AH, NBUCKET])
        line = ph.sb("line", [AH, 3 * P])
        zero = ph.sb("zero", [AH, P])
        col = ph.sb("col", [P, P], I32)
        coli = ph.sb("coli", [P, P], I32)
        colf = ph.sb("colf", [P, P])
        s_w, s_emb, s_rows, s_line, s_near, s_neard, s_flip = (
            ph.sem(x) for x in ("w", "emb", "rows", "line", "near", "neard", "flip"))
        s_pool, s_dve, s_ident, s_tps, s_tsb, s_linesb = (
            ph.sem(x) for x in ("pool", "dve", "ident", "tps", "tsb", "linesb"))
        jobs = []
        for m in range(6):
            jobs.append((m, core.winT, m * P))
        for m in range(2):
            jobs.append((6 + m, core.woutT, m * P))
        for m in range(6):
            jobs.append((8 + m, core.wattnT, m * P))
        for m in range(2):
            jobs.append((14 + m, core.wprojT, m * P))

        block = ph.block()

        @block.sync
        def _(sp):
            for k, (name, at, n) in enumerate((("L0_ffn_in_proj_w", 0, 6), ("L0_ffn_out_proj_w", 6, 2),
                                               ("L0_attn_W_attn", 8, 6), ("L0_attn_W_proj", 14, 2))):
                sp.dma_start(wraw[:, at:at + n, :], d[name].rearrange("(m p) c -> p m c", p=P)).then_inc(s_w, 16)
            sp.dma_start(core.wg[:, :, :], d["L0_ffn_wg"].rearrange("(k p) e -> p k e", p=P)).then_inc(s_rows, 16)
            for dst, src, n in (("ffn_v", d["L0_ffn_in_proj_b"][2 * C:3 * C], C), ("ffn_out", d["L0_ffn_out_proj_b"], C),
                                ("ln1_g", d["L0_ffn_ln1_g"], C), ("ln1_b", d["L0_ffn_ln1_b"], C),
                                ("ln2_g", d["L0_ffn_ln2_g"], C), ("ln2_b", d["L0_ffn_ln2_b"], C),
                                ("attn_v", d["L0_attn_b_attn"][2 * C:3 * C], C), ("proj", d["L0_attn_b_proj"], C)):
                sp.dma_start(core.rows[dst][:, :], row_bcast(src, n)).then_inc(s_rows, 16)
            with nc.allow_non_contiguous_dma("small transposed loads"):
                sp.dma_start(embT[:, :], d["L0_attn_rel_emb"].rearrange("b h -> h b")).then_inc(s_emb, 16)
                sp.dma_start(core.ffn_qk_b[:, :], d["L0_ffn_in_proj_b"][0:2 * C].rearrange("(j p) -> p j", p=P)).then_inc(s_emb, 16)
                sp.dma_start(core.attn_qk_b[:, :], d["L0_attn_b_attn"][0:2 * C].rearrange("(j p) -> p j", p=P)).then_inc(s_emb, 16)
            sp.wait_ge(s_linesb, 1)
            sp.dma_start(relrow, line[:, :]).then_inc(s_line, 16)
            sp.wait_ge(s_line, 16)
            for h in range(AH):
                src = bass.AP(tensor=relrow.tensor, offset=h * 3 * P, ap=[[1, P], [1, 2 * P]])
                sp.dma_start(hankel[:, h, :], src).then_inc(s_near, 16)
            sp.wait_ge(s_tsb, len(jobs) + AH // 2)
            sp.dma_start(neard.rearrange("h p k -> p h k"), toeplitz[:, :, :]).then_inc(s_neard, 16)
            sp.wait_ge(s_neard, 16)
            sp.wait_ge(s_rows, 16 * 9)

        @block.gpsimd
        def _(pool):
            nc.gpsimd.memset(core.ident[:, :], 0.0).then_inc(s_pool, 1)
            nc.gpsimd.memset(core.ones[:, :], 1.0).then_inc(s_pool, 1)
            pool.wait_ge(s_pool, 2)
            nc.gpsimd.affine_select(out=core.ident[:, :], in_=core.ident[:, :], compare_op=ALU.not_equal, fill=1.0,
                                    base=0, pattern=[[-1, P]], channel_multiplier=1).then_inc(s_ident, 1)
            nc.gpsimd.affine_select(out=core.before[:, :], in_=core.ones[:, :], compare_op=ALU.is_gt, fill=0.0,
                                    base=0, pattern=[[1, P]], channel_multiplier=-1).then_inc(s_pool, 1)
            nc.gpsimd.iota(col[:, :], pattern=[[1, P]], base=P, channel_multiplier=-1).then_inc(s_ident, 1)
            nc.gpsimd.memset(flip[:, :], 0.0).then_inc(s_pool, 1)
            pool.wait_ge(s_pool, 4)
            nc.gpsimd.affine_select(out=flip[:, :], in_=flip[:, :], compare_op=ALU.not_equal, fill=1.0,
                                    base=1 - P, pattern=[[1, P]], channel_multiplier=1).then_inc(s_flip, 1)
            nc.gpsimd.memset(core.mhalf[:, :], -0.5).then_inc(s_pool, 1)

        @block.vector
        def _(dve):
            n = [0]

            def link(ins):
                n[0] += 1
                ins.then_inc(s_dve, 1)
                dve.wait_ge(s_dve, n[0])

            link(nc.vector.memset(zero[:, :], 0.0))
            dve.wait_ge(s_emb, 48)
            link(nc.vector.tensor_scalar(rel[:, :], embT[:, :], -1.0, embT[:, NBUCKET - 1:NBUCKET], ALU.mult, ALU.add))
            for j, (b, lo) in enumerate(order):
                hi = order[j + 1][1] if j + 1 < len(order) else 2 * P
                w, at = hi - lo, 2 * P - hi
                while w:
                    step = min(w, P)
                    nc.vector.tensor_scalar(line[:, at:at + step], zero[:, 0:step], rel[:, b:b + 1], None, ALU.add)
                    at, w = at + step, w - step
            nc.vector.memset(line[:, 2 * P:3 * P], BIG).then_inc(s_linesb, 1)
            dve.wait_ge(s_ident, 2)
            link(nc.vector.tensor_copy(core.identb[:, :], core.ident[:, :]))
            link(nc.vector.tensor_scalar(coli[:, :], col[:, :], 15, None, ALU.bitwise_and))
            link(nc.vector.tensor_copy(colf[:, :], coli[:, :]))
            for h in range(FH):
                link(nc.vector.tensor_scalar(core.mask[:, h * P:(h + 1) * P], colf[:, :], 1.0, -BIG, ALU.min, ALU.mult))
            dve.wait_ge(s_rows, 16 * 9)
            link(nc.vector.tensor_scalar(core.rows["ln2_g"][:, :], core.rows["ln2_g"][:, :], 0.5, None, ALU.mult))
            link(nc.vector.tensor_scalar(core.rows["ln2_b"][:, :], core.rows["ln2_b"][:, :], 0.5, None, ALU.mult))
            for i, (_, dst, at) in enumerate(jobs):
                dve.wait_ge(s_tps, i + 1)
                nc.vector.tensor_copy(dst[:, :, at:at + P],
                                      core.ps[:, i % 4, 0:KB * P].rearrange("p (k c) -> p k c", k=KB)).then_inc(s_tsb, 1)
            for i in range(len(jobs), len(jobs) + AH // 2):
                dve.wait_ge(s_tps, i + 1)
                h = 2 * (i - len(jobs))
                nc.vector.tensor_copy(toeplitz[:, h:h + 2, :], core.ps[:, i % 4, :].rearrange(
                    "p (h k) -> p h k", h=2)).then_inc(s_tsb, 1)

        @block.tensor
        def _(pe):
            pe.wait_ge(s_ident, 1)
            pe.wait_ge(s_w, 64)
            for i, (slot, _, _) in enumerate(jobs):
                if i >= 4:
                    pe.wait_ge(s_tsb, i - 3)
                for k in range(KB):
                    mm = nc.tensor.transpose(core.ps[:, i % 4, k * P:(k + 1) * P], wraw[:, slot, k * P:(k + 1) * P],
                                             core.ident[:, :])
                mm.then_inc(s_tps, 1)
            pe.wait_ge(s_flip, 1)
            pe.wait_ge(s_near, 16 * AH)
            for i in range(len(jobs), len(jobs) + AH // 2):
                pe.wait_ge(s_tsb, i - 3)
                h = 2 * (i - len(jobs))
                nc.tensor.matmul(core.ps[:, i % 4, :], flip[:, :], hankel[:, h:h + 2, :], start=True,
                                 stop=True).then_inc(s_tps, 1)


def prepare_experts(core, d):
    nc = core.nc
    FB = FF // P
    core.w12 = core.keep("w12", [P, KB, NE * C])
    core.b12 = core.keep("b12", [P, NE * C])
    with Phase(core, "experts") as ph:
        w1 = ph.sb("w1", [P, 2, KB, FF])
        w2 = ph.sb("w2", [P, 2, FB, C])
        w1T = ph.sb("w1T", [P, FB, C])
        b1T = ph.sb("b1T", [P, NE, FB])
        b1w = ph.sb("b1w", [P, FB, P])
        b2r = ph.sb("b2r", [P, NE * C])
        s_w = [ph.sem("w0"), ph.sem("w1")]
        s_b2, s_b1, s_tps, s_tsb, s_w12ps, s_w12sb, s_b1w, s_b12ps, s_b12sb = (
            ph.sem(x) for x in ("b2", "b1", "tps", "tsb", "w12ps", "w12sb", "b1w", "b12ps", "b12sb"))
        block = ph.block()

        @block.sync
        def _(sp):
            sp.dma_start(b2r[:, :], row_bcast(d["L0_ffn_b2"].rearrange("e c -> (e c)"), NE * C)).then_inc(s_b2, 16)

            def body(e, u):
                if not under(e, 2):
                    sp.wait_ge(s_b12ps, e - 1)
                sp.dma_start(w1[:, u, :, :], d["L0_ffn_w1"][bass.ds(e, 1), :, :].rearrange(
                    "o (k p) f -> p (o k) f", p=P)).then_inc(s_w[u], 16)
                sp.dma_start(w2[:, u, :, :], d["L0_ffn_w2"][bass.ds(e, 1), :, :].rearrange(
                    "o (k p) c -> p (o k) c", p=P)).then_inc(s_w[u], 16)
            with nc.allow_non_contiguous_dma("small transposed loads"):
                for e in range(NE):
                    sp.dma_start(b1T[:, e, :], d["L0_ffn_b1"][e, :].rearrange("(k p) -> p k", p=P)).then_inc(s_b1, 16)
            groups(sp, NE, 2, 0, body)

        @block.tensor
        def _(pe):
            def body(e, u):
                half = e // 2 if isinstance(e, int) else None
                pe.wait_ge(s_w[u], (e - u) * 16 + 32)
                for q in range(4):
                    if not under(e, 1):
                        pe.wait_ge(s_tsb, e * 4 - 3 + q)
                    for fb in range(2 * q, 2 * q + 2):
                        for k in range(KB):
                            at = (fb % 2 * KB + k) * P
                            mm = nc.tensor.transpose(core.ps[:, q, at:at + P], w1[:, u, k, fb * P:(fb + 1) * P],
                                                     core.ident[:, :])
                    mm.then_inc(s_tps, 1)
                pe.wait_ge(s_tsb, e * 4 + 4)
                if not under(e, 1):
                    pe.wait_ge(s_w12sb, e)
                for k in range(KB):
                    for fb in range(FB):
                        mm = nc.tensor.matmul(core.ps[:, 4, k * C:(k + 1) * C], w1T[:, fb, k * P:(k + 1) * P],
                                              w2[:, u, fb, :], start=(fb == 0), stop=(fb == FB - 1))
                mm.then_inc(s_w12ps, 1)
                pe.wait_ge(s_b1w, e + 1)
                if not under(e, 1):
                    pe.wait_ge(s_b12sb, e)
                for fb in range(FB):
                    mm = nc.tensor.matmul(core.ps[:, 5, 0:C], b1w[:, fb, :], w2[:, u, fb, :],
                                          start=(fb == 0), stop=(fb == FB - 1))
                mm.then_inc(s_b12ps, 1)
            groups(pe, NE, 2, 0, body)

        def copy_w1T(eng, copy, e, q):
            eng.wait_ge(s_tps, e * 4 + q + 1)
            if not under(e, 1):
                eng.wait_ge(s_w12ps, e)
            copy(w1T[:, 2 * q:2 * q + 2, :], core.ps[:, q, :].rearrange("p (f c) -> p f c", f=2)).then_inc(s_tsb, 1)

        @block.scalar
        def _(act):
            def body(e, u):
                act.wait_ge(s_w12ps, e + 1)
                nc.scalar.copy(core.w12[:, :, bass.ds(e * C, C)],
                               core.ps[:, 4, :].rearrange("p (k c) -> p k c", k=KB)).then_inc(s_w12sb, 1)
            groups(act, NE, 2, 0, body)

        @block.vector
        def _(dve):
            dve.wait_ge(s_b1, 16 * NE)
            dve.wait_ge(s_b2, 16)

            def body(e, u):
                if not under(e, 1):
                    dve.wait_ge(s_b12ps, e)
                nc.vector.tensor_copy(b1w[:, :, :], b1T[:, bass.ds(e, 1), :].rearrange("p o f -> p (o f)")
                                      .unsqueeze(2).to_broadcast([P, FB, P])).then_inc(s_b1w, 1)
                for q in range(4):
                    copy_w1T(dve, nc.vector.tensor_copy, e, q)
                dve.wait_ge(s_b12ps, e + 1)
                nc.vector.tensor_tensor(core.b12[:, bass.ds(e * C, C)], core.ps[:, 5, 0:C], b2r[:, bass.ds(e * C, C)],
                                        ALU.add).then_inc(s_b12sb, 1)
            groups(dve, NE, 2, 0, body)



def ffn_attention(core, name, x, y1d, logits):
    nc = core.nc
    xg = x.rearrange("(p t) c -> p (t c)", p=P)
    y1g = y1d.rearrange("(p t) c -> p (t c)", p=P)
    with Phase(core, name) as ph:
        xin = ph.sb("xin", [P, 2, GT, C])
        xres = ph.sb("xres", [P, 2, GT, C])
        xT = ph.sb("xT", [P, KB, GW])
        qT = ph.sb("qT", [P, 2, 2, GW])
        kT = ph.sb("kT", [P, 2, FH, GW])
        vv = ph.sb("vv", [P, 2, GT, C])
        prob = ph.sb("prob", [P, 2, FH, P])
        probT = ph.sb("probT", [P, FH * P])
        oT = ph.sb("oT", [P, KB, GW])
        res = ph.sb("res", [P, GT, C])
        y1 = ph.sb("y1", [P, 2, GT, C])
        y1T = ph.sb("y1T", [P, KB, GW])
        negm = ph.sb("negm", [P, 2, FH])
        rsum = ph.sb("rsum", [P, 2, FH])
        rinv = ph.sb("rinv", [P, 2, FH])
        xst, xmv, xve, xrs = ph.sb("xst", [P, GT, 6]), ph.sb("xmv", [P, GT, 2]), ph.sb("xve", [P, GT]), ph.sb("xrs", [P, GT])
        yst, ymv, yve, yrs = ph.sb("yst", [P, GT, 6]), ph.sb("ymv", [P, GT, 2]), ph.sb("yve", [P, GT]), ph.sb("yrs", [P, GT])
        s_load = [ph.sem("load0"), ph.sem("load1")]
        s_store = [ph.sem("store0"), ph.sem("store1")]
        (s_xst, s_xmv, s_xve, s_xrs, s_xn, s_xres, s_xTps, s_xTsb, s_qkps, s_qsb, s_ksb, s_vps, s_vsb,
         s_sps, s_negm, s_exp, s_rinv, s_pn, s_pTps, s_pTsb, s_ops, s_osb, s_yps, s_res, s_yst, s_ymv, s_yve, s_yrs,
         s_yn, s_ymul, s_y1, s_yTps, s_yTsb, s_lgps, s_lgsb, s_kz) = (ph.sem(x) for x in (
            "xst", "xmv", "xve", "xrs", "xn", "xres", "xTps", "xTsb", "qkps", "qsb", "ksb", "vps", "vsb",
            "sps", "negm", "exp", "rinv", "pn", "pTps", "pTsb", "ops", "osb", "yps", "res", "yst", "ymv", "yve", "yrs",
            "yn", "ymul", "y1", "yTps", "yTsb", "lgps", "lgsb", "kz"))
        bank = [core.ps[:, i, :] for i in range(8)]
        TR, QK, VY, SC, PT, OO = (0, 1), 2, 3, (4, 5), 6, 7
        block = ph.block()

        @block.sync
        def _(sp):
            def store(n, u):
                sp.wait_ge(s_y1, n + 1)
                sp.dma_start(y1g[:, bass.ds(n * GT * C, GT * C)], y1[:, u, :, :].rearrange(
                    "p t c -> p (t c)")).then_inc(s_store[u], 16)

            def body(n, u):
                if not under(n, 2):
                    sp.wait_ge(s_xres, n - 1)
                    sp.wait_ge(s_xTps, 2 * n - 2)
                sp.dma_start(xin[:, u, :, :].rearrange("p t c -> p (t c)"),
                             xg[:, bass.ds(n * GT * C, GT * C)]).then_inc(s_load[u], 16)
                if not under(n, 3):
                    store(n - 3, 1 - u)
            groups(sp, NG, 4, 0, body)
            for n in range(NG - 3, NG):
                store(n, n % 2)
            for u in range(2):
                sp.wait_ge(s_store[u], 16 * (NG // 2))

        @block.tensor
        def _(pe):
            def transpose_x(n, u):
                pe.wait_ge(s_xn, n + 1)
                if not under(n, 1):
                    pe.wait_ge(s_xTsb, 2 * n)
                if not under(n, 3):
                    pe.wait_ge(s_yTsb, 2 * (n - 2))
                for k in range(KB):
                    for t in range(GT):
                        mm = nc.tensor.transpose(bank[TR[k]][:, t * P:(t + 1) * P], xin[:, u, t, k * P:(k + 1) * P],
                                                 core.ident[:, :])
                    mm.then_inc(s_xTps, 1)

            def project_qk(n, j, logits_before):
                if j == 0:
                    pe.wait_ge(s_xTsb, 2 * n + 2)
                    if not under(n, 1):
                        pe.wait_ge(s_ksb, 2 * n)
                elif j == 1:
                    pe.wait_ge(s_qsb, 2 * n + 1)
                elif j == 2:
                    pe.wait_ge(s_qsb, 2 * n + 2)
                else:
                    pe.wait_ge(s_ksb, 2 * n + 1)
                    if logits_before:
                        pe.wait_ge(s_lgsb, n - 1)
                for k in range(KB):
                    mm = nc.tensor.matmul(bank[QK], core.winT[:, k, j * P:(j + 1) * P], xT[:, k, :],
                                          start=(k == 0), stop=(k == KB - 1))
                mm.then_inc(s_qkps, 1)

            def project_v(n, h):
                if h == 0:
                    if not under(n, 2):
                        pe.wait_ge(s_res, 2 * (n - 1))
                    elif n == 1:
                        pe.wait_ge(s_vsb, 2)
                else:
                    if not under(n, 1):
                        pe.wait_ge(s_res, 2 * n - 1)
                    else:
                        pe.wait_ge(s_vsb, 1)
                for t in (2 * h, 2 * h + 1):
                    for k in range(KB):
                        mm = nc.tensor.matmul(bank[VY][:, (t % 2) * C:(t % 2 + 1) * C], xT[:, k, t * P:(t + 1) * P],
                                              core.winT[:, k, 2 * C:3 * C], start=(k == 0), stop=(k == KB - 1))
                mm.then_inc(s_vps, 1)

            def scores(n, u, t):
                if t == 0:
                    pe.wait_ge(s_qsb, 2 * n + 2)
                    pe.wait_ge(s_ksb, 2 * n + 2)
                if not (under(n, 1) and t < 2):
                    pe.wait_ge(s_exp, 4 * n + t - 1)
                nc.tensor.matmul(bank[SC[t % 2]], core.identb[:, :], core.mask[:, :], start=True, stop=False,
                                 skip_group_check=True)
                for h in range(FH):
                    mm = nc.tensor.matmul(bank[SC[t % 2]][:, h * P:(h + 1) * P], qT[:, u, h // 2, t * P:(t + 1) * P],
                                          kT[:, u, h, t * P:(t + 1) * P], start=False, stop=(h == FH - 1),
                                          skip_group_check=True)
                mm.then_inc(s_sps, 1)

            def transpose_p(n, t):
                pe.wait_ge(s_pn, 4 * n + t + 1)
                if not (under(n, 1) and t < 1):
                    pe.wait_ge(s_pTsb, 4 * n + t)
                for h in range(FH):
                    mm = nc.tensor.transpose(bank[PT][:, h * P:(h + 1) * P], prob[:, t % 2, h, :], core.ident[:, :])
                mm.then_inc(s_pTps, 1)

            def weigh_v(n, u, t):
                pe.wait_ge(s_pTsb, 4 * n + t + 1)
                pe.wait_ge(s_vsb, 2 * n + t // 2 + 1)
                if not (under(n, 1) and t < 1):
                    pe.wait_ge(s_osb, 4 * n + t)
                for h in range(FH):
                    a = h % 2 * FD
                    mm = nc.tensor.matmul(bank[OO][a:a + FD, (h // 2) * P:(h // 2 + 1) * P],
                                          vv[:, u, t, h * FD:(h + 1) * FD], probT[:, h * P:(h + 1) * P],
                                          start=True, stop=True)
                mm.then_inc(s_ops, 1)

            def project_out(n, h, last):
                pe.wait_ge(s_osb, 4 * n + 2 * h + 2)
                if not last:
                    pe.wait_ge(s_vsb, 2 * n + 3 + h)
                elif h == 0:
                    pe.wait_ge(s_res, 2 * n)
                else:
                    pe.wait_ge(s_res, 2 * n + 1)
                for t in (2 * h, 2 * h + 1):
                    for k in range(KB):
                        mm = nc.tensor.matmul(bank[VY][:, (t % 2) * C:(t % 2 + 1) * C], oT[:, k, t * P:(t + 1) * P],
                                              core.woutT[:, k, :], start=(k == 0), stop=(k == KB - 1))
                mm.then_inc(s_yps, 1)

            def transpose_y(n, u, nxt):
                pe.wait_ge(s_y1, n + 1)
                if nxt:
                    pe.wait_ge(s_xTsb, 2 * (n + 3))
                elif not under(n, 1):
                    pe.wait_ge(s_xTsb, 2 * NG)
                    pe.wait_ge(s_yTsb, 2 * n)
                for k in range(KB):
                    for t in range(GT):
                        mm = nc.tensor.transpose(bank[TR[k]][:, t * P:(t + 1) * P],
                                                 y1[:, u, t, k * P:(k + 1) * P], core.ident[:, :])
                    mm.then_inc(s_yTps, 1)

            def gate_logits(n, nxt):
                pe.wait_ge(s_yTsb, 2 * n + 2)
                if nxt:
                    pe.wait_ge(s_ksb, 2 * (n + 2) + 1)
                else:
                    pe.wait_ge(s_ksb, 2 * NG)
                    pe.wait_ge(s_lgsb, n)
                for t in range(GT):
                    for k in range(KB):
                        mm = nc.tensor.matmul(bank[QK][:, t * NE:(t + 1) * NE], y1T[:, k, t * P:(t + 1) * P],
                                              core.wg[:, k, :], start=(k == 0), stop=(k == KB - 1))
                mm.then_inc(s_lgps, 1)

            transpose_x(0, 0)
            for j in range(4):
                project_qk(0, j, False)
            project_v(0, 0)
            project_v(0, 1)
            pe.wait_ge(s_kz, 1)

            def body(n, u):
                nxt = not (isinstance(n, int) and n == NG - 1)
                prev = not under(n, 1)
                scores(n, u, 0)
                scores(n, u, 1)
                if nxt:
                    transpose_x(n + 1, 1 - u)
                transpose_p(n, 0)
                if nxt:
                    project_qk(n + 1, 0, False)
                weigh_v(n, u, 0)
                scores(n, u, 2)
                if nxt:
                    project_qk(n + 1, 1, False)
                transpose_p(n, 1)
                if prev:
                    transpose_y(n - 1, 1 - u, nxt)
                weigh_v(n, u, 1)
                scores(n, u, 3)
                if nxt:
                    project_qk(n + 1, 2, False)
                transpose_p(n, 2)
                if prev:
                    gate_logits(n - 1, nxt)
                weigh_v(n, u, 2)
                if nxt:
                    project_qk(n + 1, 3, prev)
                transpose_p(n, 3)
                if nxt:
                    project_v(n + 1, 0)
                weigh_v(n, u, 3)
                project_out(n, 0, not nxt)
                if nxt:
                    project_v(n + 1, 1)
                project_out(n, 1, not nxt)
            groups(pe, NG, 2, 2, body)
            transpose_y(NG - 1, (NG - 1) % 2, False)
            gate_logits(NG - 1, False)

        @block.scalar
        def _(act):
            def exps(n, t):
                act.wait_ge(s_negm, 4 * n + t + 1)
                for h in range(FH):
                    ins = nc.scalar.activation(prob[:, t % 2, h, :], bank[SC[t % 2]][:, h * P:(h + 1) * P], ACT.Exp,
                                               bias=negm[:, t % 2, h:h + 1], scale=1.0,
                                               accum_out=rsum[:, t % 2, h:h + 1])
                ins.then_inc(s_exp, 1)

            def xT_out(n):
                for k in range(KB):
                    act.wait_ge(s_xTps, 2 * n + k + 1)
                    nc.scalar.copy(xT[:, k, :], bank[TR[k]]).then_inc(s_xTsb, 1)

            def yT_out(n):
                for k in range(KB):
                    act.wait_ge(s_yTps, 2 * n + k + 1)
                    nc.scalar.copy(y1T[:, k, :], bank[TR[k]]).then_inc(s_yTsb, 1)

            def k_out(n, u, j):
                act.wait_ge(s_qkps, 4 * n + j + 1)
                for a in range(2):
                    r = slice(a * FD, (a + 1) * FD)
                    ins = nc.scalar.activation(kT[r, u, 2 * (j - 2) + a, :], bank[QK][r, :], ACT.Identity,
                                               bias=core.ffn_qk_b[r, j:j + 1], scale=1.0)
                ins.then_inc(s_ksb, 1)

            def o_out(n, t):
                act.wait_ge(s_ops, 4 * n + t + 1)
                nc.scalar.copy(oT[:, :, t * P:(t + 1) * P], bank[OO][:, 0:KB * P].rearrange(
                    "p (k c) -> p k c", k=KB)).then_inc(s_osb, 1)

            act.wait_ge(s_kz, 1)
            xT_out(0)
            k_out(0, 0, 2)
            k_out(0, 0, 3)

            def body(n, u):
                nxt = not (isinstance(n, int) and n == NG - 1)
                exps(n, 0)
                exps(n, 1)
                if nxt:
                    xT_out(n + 1)
                o_out(n, 0)
                exps(n, 2)
                if not under(n, 1):
                    yT_out(n - 1)
                o_out(n, 1)
                exps(n, 3)
                if nxt:
                    k_out(n + 1, 1 - u, 2)
                o_out(n, 2)
                if nxt:
                    k_out(n + 1, 1 - u, 3)
                o_out(n, 3)
            groups(act, NG, 2, 2, body)
            yT_out(NG - 1)

        @block.vector
        def _(dve):
            def x_stats(n, u):
                dve.wait_ge(s_load[u], (n - u) * 8 + 16)
                for t in range(GT):
                    ins = nc.vector.bn_stats(xst[:, t, :], xin[:, u, t, :])
                ins.then_inc(s_xst, 1)
                wait_apart(dve, s_xst, n + 1)
                for t in range(GT):
                    ins = nc.vector.bn_aggr(xmv[:, t, :], xst[:, t, :])
                ins.then_inc(s_xmv, 1)
                dve.wait_ge(s_xmv, n + 1)
                nc.vector.tensor_scalar(xve[:, :], xmv[:, :, 1], EPS, None, ALU.add).then_inc(s_xve, 1)

            def x_norm(n, u):
                dve.wait_ge(s_xrs, n + 1)
                for t in range(GT):
                    ins = nc.vector.tensor_scalar(xin[:, u, t, :], xin[:, u, t, :], xmv[:, t, 0:1], xrs[:, t:t + 1],
                                                  ALU.subtract, ALU.mult)
                ins.then_inc(s_xn, 1)

            def y_stats(n):
                dve.wait_ge(s_res, 2 * n + 2)
                for t in range(GT):
                    ins = nc.vector.bn_stats(yst[:, t, :], res[:, t, :])
                ins.then_inc(s_yst, 1)
                wait_apart(dve, s_yst, n + 1)
                for t in range(GT):
                    ins = nc.vector.bn_aggr(ymv[:, t, :], yst[:, t, :])
                ins.then_inc(s_ymv, 1)
                dve.wait_ge(s_ymv, n + 1)
                nc.vector.tensor_scalar(yve[:, :], ymv[:, :, 1], EPS, None, ALU.add).then_inc(s_yve, 1)

            def y_norm(n, u):
                dve.wait_ge(s_yrs, n + 1)
                if not under(n, 2):
                    dve.wait_ge(s_store[u], (n - u) * 8)
                    dve.wait_ge(s_yTps, 2 * (n - 1))
                for t in range(GT):
                    ins = nc.vector.tensor_scalar(y1[:, u, t, :], res[:, t, :], ymv[:, t, 0:1], yrs[:, t:t + 1],
                                                  ALU.subtract, ALU.mult)
                ins.then_inc(s_yn, 1)

            def maxima(n, t):
                dve.wait_ge(s_sps, 4 * n + t + 1)
                nc.vector.tensor_reduce(negm[:, t % 2, :], bank[SC[t % 2]].rearrange("p (h c) -> p h c", h=FH),
                                        AX.X, ALU.max, negate=True).then_inc(s_negm, 1)

            def inverses(n, t):
                dve.wait_ge(s_exp, 4 * n + t + 1)
                nc.vector.reciprocal(rinv[:, t % 2, :], rsum[:, t % 2, :]).then_inc(s_rinv, 1)

            def pT_out(n, t):
                dve.wait_ge(s_pTps, 4 * n + t + 1)
                nc.vector.tensor_copy(probT[:, :], bank[PT]).then_inc(s_pTsb, 1)

            def q_out(n, u, j):
                dve.wait_ge(s_qkps, 4 * n + j + 1)
                nc.vector.tensor_scalar(qT[:, u, j, :], bank[QK], core.ffn_qk_b[:, j:j + 1], FD ** -0.5,
                                        ALU.add, ALU.mult).then_inc(s_qsb, 1)

            def v_out(n, u, h):
                dve.wait_ge(s_vps, 2 * n + h + 1)
                nc.vector.tensor_tensor(vv[:, u, 2 * h:2 * h + 2, :], bank[VY].rearrange("p (t c) -> p t c", t=2),
                                        over(core.rows["ffn_v"][:, :], 2, 1), ALU.add).then_inc(s_vsb, 1)

            def y_out(n, u, h):
                dve.wait_ge(s_yps, 2 * n + h + 1)
                dve.wait_ge(s_xres, n + 1)
                nc.vector.tensor_tensor(res[:, 2 * h:2 * h + 2, :], bank[VY].rearrange("p (t c) -> p t c", t=2),
                                        xres[:, u, 2 * h:2 * h + 2, :], ALU.add).then_inc(s_res, 1)

            def logits_out(n):
                dve.wait_ge(s_lgps, n + 1)
                nc.vector.tensor_copy(logits[:, bass.ds(n * GT, GT), :], bank[QK][:, 0:GT * NE].rearrange(
                    "p (t e) -> p t e", t=GT)).then_inc(s_lgsb, 1)

            nc.vector.memset(kT[:, :, :, :], 0.0).then_inc(s_kz, 1)
            x_stats(0, 0)
            x_norm(0, 0)
            q_out(0, 0, 0)
            q_out(0, 0, 1)
            v_out(0, 0, 0)
            v_out(0, 0, 1)

            def body(n, u):
                nxt = not (isinstance(n, int) and n == NG - 1)
                prev = not under(n, 1)
                if nxt:
                    x_stats(n + 1, 1 - u)
                maxima(n, 0)
                maxima(n, 1)
                if prev:
                    y_norm(n - 1, 1 - u)
                if nxt:
                    x_norm(n + 1, 1 - u)
                inverses(n, 0)
                inverses(n, 1)
                pT_out(n, 0)
                if nxt:
                    q_out(n + 1, 1 - u, 0)
                maxima(n, 2)
                if nxt:
                    q_out(n + 1, 1 - u, 1)
                pT_out(n, 1)
                inverses(n, 2)
                maxima(n, 3)
                inverses(n, 3)
                pT_out(n, 2)
                if prev:
                    logits_out(n - 1)
                pT_out(n, 3)
                if nxt:
                    v_out(n + 1, 1 - u, 0)
                y_out(n, u, 0)
                if nxt:
                    v_out(n + 1, 1 - u, 1)
                y_out(n, u, 1)
                y_stats(n)
            groups(dve, NG, 2, 2, body)
            y_norm(NG - 1, (NG - 1) % 2)
            logits_out(NG - 1)

        @block.gpsimd
        def _(pool):
            def x_rstd(n):
                pool.wait_ge(s_xve, n + 1)
                nc.gpsimd.tensor_tensor(xrs[:, :], xve[:, :], core.mhalf[:, :], ALU.pow).then_inc(s_xrs, 1)

            def y_rstd(n):
                pool.wait_ge(s_yve, n + 1)
                nc.gpsimd.tensor_tensor(yrs[:, :], yve[:, :], core.mhalf[:, :], ALU.pow).then_inc(s_yrs, 1)

            def normalise(n, t):
                pool.wait_ge(s_rinv, 4 * n + t + 1)
                nc.gpsimd.tensor_tensor(prob[:, t % 2, :, :], prob[:, t % 2, :, :], over(rinv[:, t % 2, :], P, 2),
                                        ALU.mult).then_inc(s_pn, 1)

            def y_scale(n, u):
                pool.wait_ge(s_yn, n + 1)
                nc.gpsimd.tensor_tensor(y1[:, u, :, :], y1[:, u, :, :], over(core.rows["ln1_g"][:, :], GT, 1),
                                        ALU.mult).then_inc(s_ymul, 1)

            def y_shift(n, u):
                pool.wait_ge(s_ymul, n + 1)
                nc.gpsimd.tensor_tensor(y1[:, u, :, :], y1[:, u, :, :], over(core.rows["ln1_b"][:, :], GT, 1),
                                        ALU.add).then_inc(s_y1, 1)

            def x_bias(n, u):
                pool.wait_ge(s_xn, n + 1)
                if not under(n, 2):
                    pool.wait_ge(s_res, 2 * (n - 1))
                nc.gpsimd.tensor_tensor(xres[:, u, :, :], xin[:, u, :, :], over(core.rows["ffn_out"][:, :], GT, 1),
                                        ALU.add).then_inc(s_xres, 1)

            x_rstd(0)
            x_bias(0, 0)

            def body(n, u):
                nxt = not (isinstance(n, int) and n == NG - 1)
                prev = not under(n, 1)
                if nxt:
                    x_rstd(n + 1)
                normalise(n, 0)
                if prev:
                    y_scale(n - 1, 1 - u)
                normalise(n, 1)
                if prev:
                    y_shift(n - 1, 1 - u)
                normalise(n, 2)
                if nxt:
                    x_bias(n + 1, 1 - u)
                normalise(n, 3)
                y_rstd(n)
            groups(pool, NG, 2, 2, body)
            y_scale(NG - 1, (NG - 1) % 2)
            y_shift(NG - 1, (NG - 1) % 2)



def route(core, name, logits, slot, gate):
    nc = core.nc
    with Phase(core, name) as ph:
        def tile(n, *shape, dt=F32):
            return ph.sb(n, [P, *shape], dt)
        mx, se, first, keep, loc, rank, drop, dscan, t2, t3 = (tile(n, TILES) for n in (
            "mx", "se", "first", "keep", "loc", "rank", "drop", "dscan", "t2", "t3"))
        dif, ex, cand = (tile(n, TILES, NE) for n in ("dif", "ex", "cand"))
        hot, scan, a3, b3 = (tile(n, NE, TILES) for n in ("hot", "scan", "a3", "b3"))
        onest = tile("onest", TILES)
        eidx, ebase, tot, cnt, free, fend, fbeg, off = (tile(n, NE) for n in (
            "eidx", "ebase", "tot", "cnt", "free", "fend", "fbeg", "off"))
        ei = tile("ei", NE, dt=I32)
        rowtot = tile("rowtot", NE + 1)
        base = tile("base", NE + 1)
        s_dve, s_iota, s_dif, s_ex, s_rt, s_base, s_drt, s_dbase = (ph.sem(x) for x in (
            "dve", "iota", "dif", "ex", "rt", "base", "drt", "dbase"))
        bank = [core.ps[:, i, :] for i in range(8)]
        block = ph.block()

        @block.gpsimd
        def _(pool):
            nc.gpsimd.iota(ei[:, :], pattern=[[1, NE]], base=0, channel_multiplier=0).then_inc(s_iota, 1)

        @block.scalar
        def _(act):
            act.wait_ge(s_dif, 1)
            nc.scalar.activation(ex[:, :, :], dif[:, :, :], ACT.Exp).then_inc(s_ex, 1)

        @block.tensor
        def _(pe):
            pe.wait_ge(s_rt, 1)
            nc.tensor.matmul(bank[0][:, 0:NE], core.before[:, :], rowtot[:, 0:NE], start=True, stop=True)
            nc.tensor.matmul(bank[1][:, 0:NE], core.ones[:, :], rowtot[:, 0:NE], start=True, stop=True).then_inc(s_base, 1)
            pe.wait_ge(s_drt, 1)
            nc.tensor.matmul(bank[2][:, 0:1], core.before[:, :], rowtot[:, NE:NE + 1], start=True, stop=True).then_inc(s_dbase, 1)

        @block.vector
        def _(dve):
            n = [0]

            def link(ins):
                n[0] += 1
                ins.then_inc(s_dve, 1)
                dve.wait_ge(s_dve, n[0])

            V = nc.vector
            link(V.tensor_reduce(mx[:, :], logits[:, :, :], AX.X, ALU.max))
            V.tensor_tensor(dif[:, :, :], logits[:, :, :], over(mx[:, :], NE, 2), ALU.subtract).then_inc(s_dif, 1)
            dve.wait_ge(s_iota, 1)
            link(V.tensor_copy(eidx[:, :], ei[:, :]))
            link(V.tensor_scalar(ebase[:, :], eidx[:, :], float(CAP), None, ALU.mult))
            link(V.memset(onest[:, :], 1.0))
            dve.wait_ge(s_dif, 1)
            link(V.tensor_scalar(cand[:, :, :], dif[:, :, :], 0.0, -float(NE), ALU.is_ge, ALU.mult))
            link(V.tensor_tensor(cand[:, :, :], cand[:, :, :], over(eidx[:, :], TILES, 1), ALU.add))
            link(V.tensor_reduce(first[:, :], cand[:, :, :], AX.X, ALU.min))
            link(V.tensor_scalar(first[:, :], first[:, :], float(NE), None, ALU.add))
            link(V.tensor_tensor(hot[:, :, :], over(first[:, :], NE, 1), over(eidx[:, :], TILES, 2), ALU.is_equal))
            for e in range(NE):
                V.tensor_tensor_scan(scan[:, e, :], onest[:, :], hot[:, e, :], 0.0, ALU.mult, ALU.add)
            link(V.memset(t2[:, :], 0.0))
            V.tensor_copy(rowtot[:, 0:NE], scan[:, :, TILES - 1]).then_inc(s_rt, 1)
            dve.wait_ge(s_base, 1)
            link(V.tensor_copy(base[:, 0:NE], bank[0][:, 0:NE]))
            link(V.tensor_copy(tot[:, :], bank[1][:, 0:NE]))
            link(V.tensor_tensor(a3[:, :, :], scan[:, :, :], over(base[:, 0:NE], TILES, 2), ALU.add))
            link(V.tensor_tensor(a3[:, :, :], a3[:, :, :], hot[:, :, :], ALU.mult))
            link(V.tensor_reduce(loc[:, :], a3[:, :, :].rearrange("p e t -> p t e"), AX.X, ALU.add))
            link(V.tensor_scalar(loc[:, :], loc[:, :], -1.0, None, ALU.add))
            link(V.tensor_scalar(keep[:, :], loc[:, :], float(CAP), None, ALU.is_lt))
            link(V.tensor_scalar(drop[:, :], keep[:, :], -1.0, 1.0, ALU.mult, ALU.add))
            link(V.tensor_tensor_scan(dscan[:, :], onest[:, :], drop[:, :], 0.0, ALU.mult, ALU.add))
            V.tensor_copy(rowtot[:, NE:NE + 1], dscan[:, TILES - 1:TILES]).then_inc(s_drt, 1)
            link(V.tensor_scalar(cnt[:, :], tot[:, :], float(CAP), None, ALU.min))
            link(V.tensor_scalar(free[:, :], cnt[:, :], -1.0, float(CAP), ALU.mult, ALU.add))
            link(V.tensor_tensor_scan(fend[:, :], onest[:, 0:NE], free[:, :], 0.0, ALU.mult, ALU.add))
            link(V.tensor_tensor(fbeg[:, :], fend[:, :], free[:, :], ALU.subtract))
            link(V.tensor_tensor(off[:, :], ebase[:, :], cnt[:, :], ALU.add))
            link(V.tensor_tensor(off[:, :], off[:, :], fbeg[:, :], ALU.subtract))
            dve.wait_ge(s_ex, 1)
            link(V.tensor_reduce(se[:, :], ex[:, :, :], AX.X, ALU.add))
            link(V.reciprocal(se[:, :], se[:, :]))
            link(V.tensor_tensor(gate[:, :], se[:, :], keep[:, :], ALU.mult))
            dve.wait_ge(s_dbase, 1)
            link(V.tensor_copy(base[:, NE:NE + 1], bank[2][:, 0:1]))
            link(V.tensor_scalar(rank[:, :], dscan[:, :], base[:, NE:NE + 1], -1.0, ALU.add, ALU.add))
            link(V.tensor_tensor(a3[:, :, :], over(rank[:, :], NE, 1), over(fbeg[:, :], TILES, 2), ALU.is_ge))
            link(V.tensor_tensor(b3[:, :, :], over(rank[:, :], NE, 1), over(fend[:, :], TILES, 2), ALU.is_lt))
            link(V.tensor_tensor(a3[:, :, :], a3[:, :, :], b3[:, :, :], ALU.mult))
            link(V.tensor_tensor(a3[:, :, :], a3[:, :, :], over(off[:, :], TILES, 2), ALU.mult))
            link(V.tensor_reduce(t2[:, :], a3[:, :, :].rearrange("p e t -> p t e"), AX.X, ALU.add))
            link(V.tensor_tensor(t2[:, :], t2[:, :], rank[:, :], ALU.add))
            link(V.tensor_tensor(t2[:, :], t2[:, :], drop[:, :], ALU.mult))
            link(V.scalar_tensor_tensor(out=t3[:, :], in0=first[:, :], scalar=float(CAP), in1=loc[:, :],
                                        op0=ALU.mult, op1=ALU.add))
            link(V.tensor_tensor(t3[:, :], t3[:, :], keep[:, :], ALU.mult))
            link(V.tensor_tensor(t3[:, :], t3[:, :], t2[:, :], ALU.add))
            link(V.tensor_copy(slot[:, :], t3[:, :]))



def dispatch(core, name, y1d, disp, slot, base):
    nc = core.nc
    RING = 4
    y1g = y1d.rearrange("(p t) c -> p (t c)", p=P)
    with Phase(core, name) as ph:
        ring = ph.sb("ring", [P, RING, GT, C])
        s_load = [ph.sem(f"load{i}") for i in range(RING)]
        s_sent = core.indirect[0:RING]
        block = ph.block()

        @block.sync
        def _(sp):
            for n in range(NG):
                if n >= RING:
                    sp.wait_ge(s_sent[n % RING], base + 16 * GT * (n // RING))
                sp.dma_start(ring[:, n % RING, :, :].rearrange("p t c -> p (t c)"),
                             y1g[:, n * GT * C:(n + 1) * GT * C]).then_inc(s_load[n % RING], 16)

        @block.gpsimd
        def _(pool):
            for n in range(NG):
                pool.wait_ge(s_load[n % RING], 16 * (n // RING + 1))
                for t in range(GT):
                    i = n * GT + t
                    pool.indirect_dma_start(disp, bass.IndirectOffsetOnAxis(ap=slot[:, i:i + 1], axis=0),
                                            ring[:, n % RING, t, :], None).then_inc(s_sent[n % RING], 16)
            for r in range(RING):
                pool.wait_ge(s_sent[r], base + 16 * TILES // RING)


def experts(core, name, disp, zd):
    nc = core.nc
    with Phase(core, name) as ph:
        xs = ph.sb("xs", [P, 2, GT, C])
        xT = ph.sb("xT", [P, KB, GW])
        z = ph.sb("z", [P, 2, GT, C])
        s_load = [ph.sem("load0"), ph.sem("load1")]
        s_store = [ph.sem("store0"), ph.sem("store1")]
        s_tps, s_tsb0, s_tsb1, s_zps, s_zsb = (ph.sem(x) for x in ("tps", "tsb0", "tsb1", "zps", "zsb"))
        bank = [core.ps[:, i, :] for i in range(8)]
        rows = disp.rearrange("(g p t) c -> g p (t c)", p=P, t=GT)
        outs = zd.rearrange("(g p t) c -> g p (t c)", p=P, t=GT)
        block = ph.block()

        @block.sync
        def _(sp):
            def body(n, u):
                if not under(n, 2):
                    sp.wait_ge(s_tps, 2 * (n - 1))
                sp.dma_start(xs[:, u, :, :].rearrange("p t c -> p (t c)"), rows[bass.ds(n, 1), :, :].rearrange(
                    "o p c -> p (o c)")).then_inc(s_load[u], 16)
            groups(sp, NG, 2, 0, body)

        @block.tensor
        def _(pe):
            def transposes(n, u):
                pe.wait_ge(s_load[u], (n - u) * 8 + 16)
                if not under(n, 2):
                    pe.wait_ge(s_tsb0, n - 1)
                    pe.wait_ge(s_tsb1, n - 1)
                for k in range(KB):
                    for t in range(GT):
                        mm = nc.tensor.transpose(bank[2 * u + k][:, t * P:(t + 1) * P], xs[:, u, t, k * P:(k + 1) * P],
                                                 core.ident[:, :])
                    mm.then_inc(s_tps, 1)

            def products(n, u):
                pe.wait_ge(s_tsb0, n + 1)
                pe.wait_ge(s_tsb1, n + 1)
                for h in range(2):
                    if not under(n, 1):
                        pe.wait_ge(s_zsb, 2 * n - 1 + h)
                    for t in (2 * h, 2 * h + 1):
                        for k in range(KB):
                            mm = nc.tensor.matmul(bank[4 + h][:, (t % 2) * C:(t % 2 + 1) * C],
                                                  xT[:, k, t * P:(t + 1) * P],
                                                  core.w12[:, k, bass.ds((n - u) * (C // 2), C)],
                                                  start=(k == 0), stop=(k == KB - 1))
                    mm.then_inc(s_zps, 1)

            transposes(0, 0)

            def body(n, u):
                if not (isinstance(n, int) and n == NG - 1):
                    transposes(n + 1, 1 - u)
                products(n, u)
            groups(pe, NG, 2, 2, body)

        @block.scalar
        def _(act):
            def body(n, u):
                act.wait_ge(s_tps, 2 * n + 1)
                if not under(n, 1):
                    act.wait_ge(s_zps, 2 * n)
                nc.scalar.copy(xT[:, 0, :], bank[2 * u]).then_inc(s_tsb0, 1)
                act.wait_ge(s_zsb, 2 * n + 2)
                act.dma_start(outs[bass.ds(n, 1), :, :].rearrange("o p c -> p (o c)"),
                              z[:, u, :, :].rearrange("p t c -> p (t c)")).then_inc(s_store[u], 16)
            groups(act, NG, 2, 0, body)
            for u in range(2):
                act.wait_ge(s_store[u], 16 * (NG // 2))

        @block.vector
        def _(dve):
            def body(n, u):
                dve.wait_ge(s_tps, 2 * n + 2)
                if not under(n, 1):
                    dve.wait_ge(s_zps, 2 * n)
                nc.vector.tensor_copy(xT[:, 1, :], bank[2 * u + 1]).then_inc(s_tsb1, 1)
                if not under(n, 2):
                    dve.wait_ge(s_store[u], (n - u) * 8)
                for h in range(2):
                    dve.wait_ge(s_zps, 2 * n + h + 1)
                    nc.vector.tensor_tensor(z[:, u, 2 * h:2 * h + 2, :],
                                            bank[4 + h].rearrange("p (t c) -> p t c", t=2),
                                            over(core.b12[:, bass.ds((n - u) * (C // 2), C)], 2, 1),
                                            ALU.add).then_inc(s_zsb, 1)
            groups(dve, NG, 2, 0, body)


def combine(core, name, x, y1d, zd, out, slot, gate, base):
    nc = core.nc
    RING = 4
    grp = [a.rearrange("(p t) c -> p (t c)", p=P) for a in (x, y1d, out)]
    with Phase(core, name) as ph:
        zr = ph.sb("zr", [P, RING, GT, C])
        y = ph.sb("y", [P, RING, GT, C])
        xr = ph.sb("xr", [P, RING, GT, C])
        res = ph.sb("res", [P, RING, GT, C])
        st = ph.sb("st", [P, GT, 6])
        mv, ve, rs, nb = (ph.sb(n, s) for n, s in (("mv", [P, 2, GT, 2]), ("ve", [P, 2, GT]),
                                                   ("rs", [P, 2, GT]), ("nb", [P, 2, GT])))
        s_got = core.indirect[4:4 + RING]
        s_ld = [ph.sem(f"ld{i}") for i in range(RING)]
        s_out = [ph.sem(f"out{i}") for i in range(RING)]
        s_sum, s_st, s_mv, s_ve, s_sd, s_rs, s_norm, s_inv, s_xb, s_fin = (ph.sem(n) for n in (
            "sum", "st", "mv", "ve", "sd", "rs", "norm", "inv", "xb", "fin"))
        s_scaled = ph.sem("scaled")
        block = ph.block()

        @block.gpsimd
        def _(pool):
            for n in range(NG):
                if n >= RING:
                    pool.wait_ge(s_sum, n - RING + 1)
                for t in range(GT):
                    i = n * GT + t
                    pool.indirect_dma_start(zr[:, n % RING, t, :], None, zd,
                                            bass.IndirectOffsetOnAxis(ap=slot[:, i:i + 1], axis=0)
                                            ).then_inc(s_got[n % RING], 16)

        def quads(eng, body):
            for n in range(RING):
                body(n, n)
            with eng.Fori(1, NG // RING - 1) as it:
                for r in range(RING):
                    body(it * RING + r, r)
            for n in range(NG - RING, NG):
                body(n, n % RING)

        @block.sync
        def _(sp):
            def store(n, r):
                sp.wait_ge(s_fin, n + 1)
                sp.dma_start(grp[2][:, bass.ds(n * GT * C, GT * C)], res[:, r, :, :].rearrange(
                    "p t c -> p (t c)")).then_inc(s_out[r], 16)

            def body(n, r):
                if not under(n, RING):
                    sp.wait_ge(s_fin, n - RING + 1)
                for src, dst in ((grp[1], y), (grp[0], xr)):
                    sp.dma_start(dst[:, r, :, :].rearrange("p t c -> p (t c)"),
                                 src[:, bass.ds(n * GT * C, GT * C)]).then_inc(s_ld[r], 16)
                if not under(n, 3):
                    store(n - 3, (r - 3) % RING)
            quads(sp, body)
            for n in range(NG - 3, NG):
                store(n, n % RING)
            for r in range(RING):
                sp.wait_ge(s_out[r], 16 * (NG // RING))

        @block.scalar
        def _(act):
            def root(n, r):
                act.wait_ge(s_ve, n + 1)
                nc.scalar.activation(ve[:, r % 2, :], ve[:, r % 2, :], ACT.Sqrt).then_inc(s_sd, 1)

            root(0, 0)

            def body(n, r):
                if not (isinstance(n, int) and n == NG - 1):
                    root(n + 1, r + 1)
                act.wait_ge(s_rs, n + 1)
                for t in range(GT):
                    ins = nc.scalar.activation(res[:, r, t, :], res[:, r, t, :], ACT.Identity,
                                               bias=nb[:, r % 2, t:t + 1], scale=rs[:, r % 2, t:t + 1])
                ins.then_inc(s_norm, 1)
            quads(act, body)

        @block.vector
        def _(dve):
            def sums(n, r):
                r = r % RING
                dve.wait_ge(s_ld[r], (n - r) * 8 + 32)
                dve.wait_ge(s_got[r], (n - r) * 16 + 16 * GT + base)
                if not under(n, RING):
                    dve.wait_ge(s_out[r], (n - r) * 4)
                for t in range(GT):
                    ins = nc.vector.scalar_tensor_tensor(out=res[:, r, t, :], in0=zr[:, r, t, :],
                                                         scalar=gate[:, bass.ds(n * GT + t, 1)],
                                                         in1=y[:, r, t, :], op0=ALU.mult, op1=ALU.add)
                ins.then_inc(s_sum, 1)
                nc.vector.tensor_tensor(xr[:, r, :, :], xr[:, r, :, :], over(core.rows["ln2_b"][:, :], GT, 1),
                                        ALU.add).then_inc(s_xb, 1)
                dve.wait_ge(s_sum, n + 1)
                for t in range(GT):
                    ins = nc.vector.bn_stats(st[:, t, :], res[:, r, t, :])
                ins.then_inc(s_st, 1)
                wait_apart(dve, s_st, n + 1)
                for t in range(GT):
                    ins = nc.vector.bn_aggr(mv[:, r % 2, t, :], st[:, t, :])
                ins.then_inc(s_mv, 1)
                dve.wait_ge(s_mv, n + 1)
                nc.vector.tensor_scalar(ve[:, r % 2, :], mv[:, r % 2, :, 1], EPS, None, ALU.add).then_inc(s_ve, 1)

            def factors(n, r):
                dve.wait_ge(s_sd, n + 1)
                if not under(n, 2):
                    dve.wait_ge(s_norm, n - 1)
                nc.vector.reciprocal(rs[:, r % 2, :], ve[:, r % 2, :]).then_inc(s_inv, 1)
                dve.wait_ge(s_inv, n + 1)
                nc.vector.scalar_tensor_tensor(out=nb[:, r % 2, :], in0=mv[:, r % 2, :, 0], scalar=-1.0,
                                               in1=rs[:, r % 2, :], op0=ALU.mult, op1=ALU.mult).then_inc(s_rs, 1)

            def scale(n, r):
                dve.wait_ge(s_norm, n + 1)
                nc.vector.tensor_tensor(res[:, r % RING, :, :], res[:, r % RING, :, :],
                                        over(core.rows["ln2_g"][:, :], GT, 1), ALU.mult).then_inc(s_scaled, 1)

            def finish(n, r):
                dve.wait_ge(s_scaled, n + 1)
                dve.wait_ge(s_xb, n + 1)
                nc.vector.tensor_tensor(res[:, r % RING, :, :], res[:, r % RING, :, :], xr[:, r % RING, :, :],
                                        ALU.add).then_inc(s_fin, 1)

            sums(0, 0)

            def body(n, r):
                factors(n, r)
                if not (isinstance(n, int) and n == NG - 1):
                    sums(n + 1, r + 1)
                if not under(n, 1):
                    scale(n - 1, r - 1)
                    finish(n - 1, r - 1)
            quads(dve, body)
            scale(NG - 1, NG - 1)
            finish(NG - 1, NG - 1)



def attention_qkv(core, x, qd, kd, vall):
    nc = core.nc
    rows = x.rearrange("(g t p) c -> g p t c", p=P, t=GT)
    with Phase(core, "qkv") as ph:
        xin = ph.sb("xin", [P, 2, GT, C])
        xT = ph.sb("xT", [P, KB, GW])
        f = ph.sb("f", [P, 4, GW])
        part = ph.sb("part", [P, 4, 3, GW], BF16)
        xst, xmv, xve, xrs = ph.sb("xst", [P, GT, 6]), ph.sb("xmv", [P, GT, 2]), ph.sb("xve", [P, GT]), ph.sb("xrs", [P, GT])
        s_load = [ph.sem("load0"), ph.sem("load1")]
        s_store = [ph.sem(f"store{j}") for j in range(4)]
        (s_xst, s_xmv, s_xve, s_xrs, s_xn, s_tps, s_tsb0, s_tsb1, s_qkps, s_f, s_hi, s_r, s_mid, s_lo, s_vps, s_vsb) = (
            ph.sem(x) for x in ("xst", "xmv", "xve", "xrs", "xn", "tps", "tsb0", "tsb1", "qkps", "f", "hi", "r",
                                "mid", "lo", "vps", "vsb"))
        bank = [core.ps[:, i, :] for i in range(8)]
        block = ph.block()

        @block.sync
        def _(sp):
            def load(n, u):
                if not under(n, 2):
                    sp.wait_ge(s_tps, 2 * (n - 1))
                sp.dma_start(xin[:, u, :, :], rows[bass.ds(n, 1), :, :, :].rearrange(
                    "o p t c -> p (o t) c")).then_inc(s_load[u], 16)

            load(0, 0)

            def body(n, u):
                if not (isinstance(n, int) and n == NG - 1):
                    load(n + 1, 1 - u)
                for j in range(4):
                    sp.wait_ge(s_lo, 4 * n + j + 1)
                    dst = (qd, kd)[j // 2][bass.ds((n - u) * P + (j % 2) * P, P), :, u * GW:(u + 1) * GW]
                    sp.dma_start(dst, part[:, j, :, :]).then_inc(s_store[j], 16)
            groups(sp, NG, 2, 2, body)
            for j in range(4):
                sp.wait_ge(s_store[j], 16 * NG)

        @block.tensor
        def _(pe):
            def transposes(n, u):
                pe.wait_ge(s_xn, n + 1)
                if not under(n, 1):
                    pe.wait_ge(s_tsb0, n)
                    pe.wait_ge(s_tsb1, n)
                for k in range(KB):
                    for t in range(GT):
                        mm = nc.tensor.transpose(bank[k][:, t * P:(t + 1) * P], xin[:, u, t, k * P:(k + 1) * P],
                                                 core.ident[:, :])
                    mm.then_inc(s_tps, 1)

            transposes(0, 0)

            def body(n, u):
                pe.wait_ge(s_tsb0, n + 1)
                pe.wait_ge(s_tsb1, n + 1)
                for j in range(4):
                    if not (under(n, 1) and j < 2):
                        pe.wait_ge(s_f, 4 * n + j - 1)
                    for k in range(KB):
                        mm = nc.tensor.matmul(bank[2 + j % 2], core.wattnT[:, k, j * P:(j + 1) * P], xT[:, k, :],
                                              start=(k == 0), stop=(k == KB - 1))
                    mm.then_inc(s_qkps, 1)
                    if j == 1 and not (isinstance(n, int) and n == NG - 1):
                        transposes(n + 1, 1 - u)
                for h in range(2):
                    if not under(n, 1):
                        pe.wait_ge(s_vsb, 2 * n - 1 + h)
                    for t in (2 * h, 2 * h + 1):
                        for k in range(KB):
                            mm = nc.tensor.matmul(bank[4 + h][:, (t % 2) * C:(t % 2 + 1) * C],
                                                  xT[:, k, t * P:(t + 1) * P], core.wattnT[:, k, 2 * C:3 * C],
                                                  start=(k == 0), stop=(k == KB - 1))
                    mm.then_inc(s_vps, 1)
            groups(pe, NG, 2, 2, body)

        @block.scalar
        def _(act):
            def body(n, u):
                act.wait_ge(s_tps, 2 * n + 1)
                if not under(n, 1):
                    act.wait_ge(s_vps, 2 * n)
                nc.scalar.copy(xT[:, 0, :], bank[0]).then_inc(s_tsb0, 1)
                for j in range(4):
                    act.wait_ge(s_f, 4 * n + j + 1)
                    if not under(n, 1):
                        act.wait_ge(s_store[j], 16 * n)
                    nc.scalar.copy(part[:, j, 0, :], f[:, j, :]).then_inc(s_hi, 1)
                    if j:
                        act.wait_ge(s_r, 4 * n + j)
                        nc.scalar.copy(part[:, j - 1, 1, :], f[:, j - 1, :]).then_inc(s_mid, 1)
                act.wait_ge(s_r, 4 * n + 4)
                nc.scalar.copy(part[:, 3, 1, :], f[:, 3, :]).then_inc(s_mid, 1)
            groups(act, NG, 2, 2, body)

        @block.vector
        def _(dve):
            def x_stats(n, u):
                dve.wait_ge(s_load[u], (n - u) * 8 + 16)
                for t in range(GT):
                    ins = nc.vector.bn_stats(xst[:, t, :], xin[:, u, t, :])
                ins.then_inc(s_xst, 1)
                wait_apart(dve, s_xst, n + 1)
                for t in range(GT):
                    ins = nc.vector.bn_aggr(xmv[:, t, :], xst[:, t, :])
                ins.then_inc(s_xmv, 1)
                dve.wait_ge(s_xmv, n + 1)
                nc.vector.tensor_scalar(xve[:, :], xmv[:, :, 1], EPS, None, ALU.add).then_inc(s_xve, 1)

            def x_norm(n, u):
                dve.wait_ge(s_xrs, n + 1)
                for t in range(GT):
                    ins = nc.vector.tensor_scalar(xin[:, u, t, :], xin[:, u, t, :], xmv[:, t, 0:1], xrs[:, t:t + 1],
                                                  ALU.subtract, ALU.mult)
                ins.then_inc(s_xn, 1)

            def value(n, j):
                dve.wait_ge(s_qkps, 4 * n + j + 1)
                if not under(n, 1):
                    dve.wait_ge(s_lo, 4 * n + j - 3)
                nc.vector.tensor_scalar(f[:, j, :], bank[2 + j % 2], core.attn_qk_b[:, j:j + 1],
                                        -(AD ** -0.5) if j < 2 else 1.0, ALU.add, ALU.mult).then_inc(s_f, 1)

            def rest(n, j):
                dve.wait_ge(s_hi, 4 * n + j + 1)
                nc.vector.tensor_tensor(f[:, j, :], f[:, j, :], part[:, j, 0, :], ALU.subtract).then_inc(s_r, 1)

            x_stats(0, 0)
            x_norm(0, 0)

            def body(n, u):
                nxt = not (isinstance(n, int) and n == NG - 1)
                dve.wait_ge(s_tps, 2 * n + 2)
                if not under(n, 1):
                    dve.wait_ge(s_vps, 2 * n)
                nc.vector.tensor_copy(xT[:, 1, :], bank[1]).then_inc(s_tsb1, 1)
                if nxt:
                    x_stats(n + 1, 1 - u)
                value(n, 0)
                if nxt:
                    x_norm(n + 1, 1 - u)
                value(n, 1)
                rest(n, 0)
                value(n, 2)
                rest(n, 1)
                value(n, 3)
                rest(n, 2)
                rest(n, 3)
                for h in range(2):
                    dve.wait_ge(s_vps, 2 * n + h + 1)
                    j = u * GT + 2 * h
                    nc.vector.tensor_tensor(
                        vall[:, bass.ds((n - u) * 2, NHG), j:j + 2, :].rearrange("p g j d -> p j g d"),
                        bank[4 + h].rearrange("p (t g d) -> p t g d", t=2, g=NHG),
                        over(core.rows["attn_v"].rearrange("p (g d) -> p g d", g=NHG), 2, 1),
                        ALU.add).then_inc(s_vsb, 1)
            groups(dve, NG, 2, 2, body)

        @block.gpsimd
        def _(pool):
            def x_rstd(n):
                pool.wait_ge(s_xve, n + 1)
                nc.gpsimd.tensor_tensor(xrs[:, :], xve[:, :], core.mhalf[:, :], ALU.pow).then_inc(s_xrs, 1)

            x_rstd(0)

            def body(n, u):
                if not (isinstance(n, int) and n == NG - 1):
                    x_rstd(n + 1)
                for j in range(4):
                    pool.wait_ge(s_mid, 4 * n + j + 1)
                    nc.gpsimd.tensor_tensor(part[:, j, 2, :], f[:, j, :], part[:, j, 1, :], ALU.subtract).then_inc(s_lo, 1)
            groups(pool, NG, 2, 2, body)



Q_PARTS = (0, 0, 0, 1, 1, 2)
K_PARTS = (0, 1, 2, 0, 1, 0)


def attention_core(core, qd, kd, neard, vall):
    nc = core.nc
    NU = B * NHG
    STEPS = QB * HG
    K6 = len(Q_PARTS) * AD

    def blk(s):
        return QB - 1 - s // HG

    def chunks(s):
        n = blk(s) + 1
        return [(0, 0, 4), (1, 4, n - 4)] if n > 4 else [(s % 2, 0, n)]

    def done(par, s):
        return sum(c[0] == par for q in range(s + 1) for c in chunks(q))

    PER = done(0, STEPS - 1)
    FAR = sum(blk(s) >= 2 for s in range(STEPS))
    with Phase(core, "attn") as ph:
        qst = ph.sb("qst", [K6, 2, HG, T], BF16)
        kst = ph.sb("kst", [K6, 2, HG, T], BF16)
        near = ph.sb("near", [P, 2, HG, 2 * P])
        vb = ph.sb("vb", [P, 2, QB, HG, 32])
        prob = ph.sb("prob", [P, 2, T])
        probT = ph.sb("probT", [P, HG + 1, QB, P])
        oT = ph.sb("oT", [P, P])
        farm = ph.sb("farm", [P, 2])
        low = ph.sb("low", [P, 2])
        rsum = ph.sb("rsum", [P, 2, HG])
        rinv = ph.sb("rinv", [P, 2, HG])
        s_load = [ph.sem("load0"), ph.sem("load1")]
        s_T = [ph.sem("T0"), ph.sem("T1")]
        s_Tsb = [ph.sem("Tsb0"), ph.sem("Tsb1")]
        (s_vz, s_vb, s_S, s_far, s_low, s_exp, s_O, s_Osb, s_Y, s_rinv, s_y) = (ph.sem(x) for x in (
            "vz", "vb", "S", "far", "low", "exp", "O", "Osb", "Y", "rinv", "y"))
        LOADS = 16 * (2 * len(Q_PARTS) + 1)
        score = [core.ps[:, 0:2, :].rearrange("p a b -> p (a b)"), core.ps[:, 2:4, :].rearrange("p a b -> p (a b)")]
        tbank = [core.ps[:, 4, :], core.ps[:, 5, :]]
        obank, ybank = core.ps[:, 6, :], core.ps[:, 7, :]

        def slot_of(s):
            return HG if s % HG == 0 and (s // HG) % 2 else s % HG

        def ahead(n, u, s):
            return (n, u, s) if s < STEPS else (n + 1, 1 - u, s - STEPS)

        def last(n):
            return isinstance(n, int) and n == NU - 1

        block = ph.block()

        @block.sync
        def _(sp):
            def body(n, u):
                if not under(n, 2):
                    sp.wait_ge(s_S, STEPS * (n - 1))
                    sp.wait_ge(s_low, STEPS * (n - 1))
                for dst, src, parts in ((qst, qd, Q_PARTS), (kst, kd, K_PARTS)):
                    for r, a in enumerate(parts):
                        sp.dma_start(dst[r * AD:(r + 1) * AD, u, :, :],
                                     src[bass.ds(n * HG * AD, HG * AD), a, :].rearrange("(h d) t -> d h t", d=AD)
                                     ).then_inc(s_load[u], 16)
                sp.dma_start(near[:, u, :, :], neard[bass.ds(n % NHG * HG, HG), :, :].rearrange(
                    "h p k -> p h k")).then_inc(s_load[u], 16)
            groups(sp, NU, 2, 0, body)

        @block.tensor
        def _(pe):
            def scores(n, u, s):
                n, u, s = ahead(n, u, s)
                i, hh = blk(s), s % HG
                if s == 0:
                    pe.wait_ge(s_load[u], (n - u) * (LOADS // 2) + LOADS)
                if not (under(n, 1) and s < 2):
                    pe.wait_ge(s_exp, STEPS * n + s - 1)
                w = (i + 1) * P
                for a in range(0, w, 512):
                    e = min(w, a + 512)
                    mm = nc.tensor.matmul(score[s % 2][:, a:e], qst[:, u, hh, i * P:(i + 1) * P], kst[:, u, hh, a:e],
                                          start=True, stop=True)
                mm.then_inc(s_S, 1)

            def transposes(n, u, s):
                pe.wait_ge(s_exp, STEPS * n + s + 1)
                for par, j0, w in chunks(s):
                    before = done(par, s) - 1
                    if not (under(n, 1) and before == 0):
                        pe.wait_ge(s_Tsb[par], PER * n + before)
                    for j in range(w):
                        mm = nc.tensor.transpose(tbank[par][:, j * P:(j + 1) * P],
                                                 prob[:, s % 2, (j0 + j) * P:(j0 + j + 1) * P], core.ident[:, :])
                    mm.then_inc(s_T[par], 1)

            def weigh_v(n, u, m):
                if m < 0:
                    n, u, m = n - 1, 1 - u, QB - 1
                i, s = QB - 1 - m, m * HG + HG - 1
                if m == 0:
                    pe.wait_ge(s_vb, n + 1)
                for par in range(2):
                    pe.wait_ge(s_Tsb[par], PER * n + done(par, s))
                if not (under(n, 1) and m == 0):
                    pe.wait_ge(s_Osb, QB * n + m)
                for j in range(i + 1):
                    for hh in range(HG):
                        mm = nc.tensor.matmul(obank[32 * hh:32 * hh + 32, 0:P], vb[:, u, j, hh, :],
                                              probT[:, slot_of(m * HG + hh), j, :], start=(j == 0), stop=(j == i))
                mm.then_inc(s_O, 1)

            def turn_back(n, m):
                if m < 0:
                    n, m = n - 1, QB - 1
                pe.wait_ge(s_Osb, QB * n + m + 1)
                if not (under(n, 1) and m == 0):
                    pe.wait_ge(s_y, QB * n + m)
                nc.tensor.transpose(ybank[:, 0:P], oT[:, :], core.ident[:, :]).then_inc(s_Y, 1)

            scores(0, 0, 0)
            scores(0, 0, 1)

            def body(n, u):
                for s in range(STEPS):
                    if not (last(n) and s + 2 >= STEPS):
                        scores(n, u, s + 2)
                    transposes(n, u, s)
                    m = s // HG - 1
                    if not (under(n, 1) and m < 0):
                        if s % HG == 0:
                            weigh_v(n, u, m)
                        if s % HG == 2:
                            turn_back(n, m)
            groups(pe, NU, 2, 2, body)
            weigh_v(NU - 1, (NU - 1) % 2, QB - 1)
            turn_back(NU - 1, QB - 1)

        @block.scalar
        def _(act):
            def exps(n, u, s):
                n, u, s = ahead(n, u, s)
                act.wait_ge(s_low, STEPS * n + s + 1)
                for par in range(2):
                    if s >= 2 and done(par, s - 2):
                        act.wait_ge(s_T[par], PER * n + done(par, s - 2))
                    elif not under(n, 1):
                        act.wait_ge(s_T[par], PER * (n - 1) + done(par, STEPS + s - 2))
                m = s // HG
                if s % HG == 0 and not (under(n, 1) and m < 2):
                    act.wait_ge(s_y, QB * n + m - 1)
                w = (blk(s) + 1) * P
                nc.scalar.activation(prob[:, s % 2, 0:w], score[s % 2][:, 0:w], ACT.Exp, bias=low[:, s % 2:s % 2 + 1],
                                     scale=-1.0, accum_out=rsum[:, m % 2, s % HG:s % HG + 1]).then_inc(s_exp, 1)

            def copy_o(n, m):
                if m < 0:
                    n, m = n - 1, QB - 1
                act.wait_ge(s_O, QB * n + m + 1)
                if not (under(n, 1) and m == 0):
                    act.wait_ge(s_Y, QB * n + m)
                nc.scalar.copy(oT[:, :], obank[:, 0:P]).then_inc(s_Osb, 1)

            exps(0, 0, 0)

            def body(n, u):
                for s in range(STEPS):
                    if not (last(n) and s + 1 >= STEPS):
                        exps(n, u, s + 1)
                    for par, j0, w in chunks(s):
                        if par == 1:
                            act.wait_ge(s_T[1], PER * n + done(1, s))
                            nc.scalar.copy(probT[:, slot_of(s), j0:j0 + w, :], tbank[1][:, 0:w * P].rearrange(
                                "p (j c) -> p j c", j=w)).then_inc(s_Tsb[1], 1)
                    if s % HG == 1 and not (under(n, 1) and s < HG):
                        copy_o(n, s // HG - 1)
            groups(act, NU, 2, 2, body)
            copy_o(NU - 1, QB - 1)

        @block.vector
        def _(dve):
            def minimum(n, u, s):
                n, u, s = ahead(n, u, s)
                i, hh = blk(s), s % HG
                if s == 0:
                    dve.wait_ge(s_load[u], (n - u) * (LOADS // 2) + LOADS)
                wait_apart(dve, s_S, STEPS * n + s + 1)
                start = BIG
                if i >= 2:
                    nc.vector.tensor_reduce(farm[:, s % 2:s % 2 + 1], score[s % 2][:, 0:(i - 1) * P], AX.X,
                                            ALU.min).then_inc(s_far, 1)
                    wait_apart(dve, s_far, FAR * n + s + 1)
                    start = farm[:, s % 2:s % 2 + 1]
                a, w = (max(i - 1, 0) * P, 2 * P) if i else (0, P)
                part = score[s % 2][:, a:a + w]
                nc.vector.tensor_tensor_reduce(out=part, in0=part, in1=near[:, u, hh, 2 * P - w:2 * P], scale=1.0,
                                               scalar=start, op0=ALU.add, op1=ALU.min,
                                               accum_out=low[:, s % 2:s % 2 + 1]).then_inc(s_low, 1)

            def finish(n, m):
                if m < 0:
                    n, m = n - 1, QB - 1
                dve.wait_ge(s_exp, STEPS * n + (m + 1) * HG)
                nc.vector.reciprocal(rinv[:, m % 2, :], rsum[:, m % 2, :]).then_inc(s_rinv, 1)
                dve.wait_ge(s_rinv, QB * n + m + 1)
                dve.wait_ge(s_Y, QB * n + m + 1)
                nc.vector.tensor_tensor(
                    vall[:, bass.ds(n, 1), QB - 1 - m, :].rearrange("p o (h d) -> p (o h) d", h=HG),
                    ybank[:, 0:P].rearrange("p (h d) -> p h d", h=HG)[:, :, 0:AD],
                    over(rinv[:, m % 2, :], AD, 2), ALU.mult).then_inc(s_y, 1)

            minimum(0, 0, 0)

            def body(n, u):
                for s in range(STEPS):
                    if not (last(n) and s + 1 >= STEPS):
                        minimum(n, u, s + 1)
                    for par, j0, w in chunks(s):
                        if par == 0:
                            dve.wait_ge(s_T[0], PER * n + done(0, s))
                            nc.vector.tensor_copy(probT[:, slot_of(s), j0:j0 + w, :], tbank[0][:, 0:w * P].rearrange(
                                "p (j c) -> p j c", j=w)).then_inc(s_Tsb[0], 1)
                    if s % HG == 3 and not (under(n, 1) and s < HG):
                        finish(n, s // HG - 1)
            groups(dve, NU, 2, 2, body)
            finish(NU - 1, QB - 1)

        @block.gpsimd
        def _(pool):
            nc.gpsimd.memset(vb[:, :, :, :, :], 0.0).then_inc(s_vz, 1)
            pool.wait_ge(s_vz, 1)

            def body(n, u):
                if not under(n, 2):
                    pool.wait_ge(s_O, QB * (n - 1))
                nc.gpsimd.tensor_copy(vb[:, u, :, :, 0:AD], vall[:, bass.ds(n, 1), :, :].rearrange(
                    "p o j (h d) -> p (o j) h d", h=HG)).then_inc(s_vb, 1)
            groups(pool, NU, 2, 0, body)


def attention_out(core, x, vall, out):
    nc = core.nc
    rows, outs = (a.rearrange("(g t p) c -> g p t c", p=P, t=GT) for a in (x, out))
    with Phase(core, "proj") as ph:
        y = ph.sb("y", [P, 2, GT, C])
        yT = ph.sb("yT", [P, KB, GW])
        xr = ph.sb("xr", [P, 2, GT, C])
        s_load = [ph.sem("load0"), ph.sem("load1")]
        s_store = [ph.sem("store0"), ph.sem("store1")]
        s_y, s_xb, s_tps, s_tsb0, s_tsb1, s_ops, s_osb = (ph.sem(x) for x in (
            "y", "xb", "tps", "tsb0", "tsb1", "ops", "osb"))
        bank = [core.ps[:, i, :] for i in range(8)]
        block = ph.block()

        @block.sync
        def _(sp):
            def body(n, u):
                if not under(n, 2):
                    sp.wait_ge(s_store[u], (n - u) * 8)
                sp.dma_start(xr[:, u, :, :], rows[bass.ds(n, 1), :, :, :].rearrange(
                    "o p t c -> p (o t) c")).then_inc(s_load[u], 16)
            groups(sp, NG, 2, 0, body)

        @block.gpsimd
        def _(pool):
            def body(n, u):
                if not under(n, 2):
                    pool.wait_ge(s_tps, 2 * (n - 1))
                nc.gpsimd.tensor_copy(y[:, u, :, :].rearrange("p t (g d) -> p t g d", g=NHG),
                                      vall[:, bass.ds((n - u) * 2, NHG), u * GT:(u + 1) * GT, :].rearrange(
                                          "p g t d -> p t g d")).then_inc(s_y, 1)
            groups(pool, NG, 2, 0, body)

        @block.tensor
        def _(pe):
            def transposes(n, u):
                pe.wait_ge(s_y, n + 1)
                if not under(n, 1):
                    pe.wait_ge(s_tsb0, n)
                    pe.wait_ge(s_tsb1, n)
                for k in range(KB):
                    for t in range(GT):
                        mm = nc.tensor.transpose(bank[k][:, t * P:(t + 1) * P], y[:, u, t, k * P:(k + 1) * P],
                                                 core.ident[:, :])
                    mm.then_inc(s_tps, 1)

            def body(n, u):
                transposes(n, u)
                pe.wait_ge(s_tsb0, n + 1)
                pe.wait_ge(s_tsb1, n + 1)
                for h in range(2):
                    if not under(n, 1):
                        pe.wait_ge(s_osb, 2 * n - 1 + h)
                    for t in (2 * h, 2 * h + 1):
                        for k in range(KB):
                            mm = nc.tensor.matmul(bank[2 + h][:, (t % 2) * C:(t % 2 + 1) * C],
                                                  yT[:, k, t * P:(t + 1) * P], core.wprojT[:, k, :],
                                                  start=(k == 0), stop=(k == KB - 1))
                    mm.then_inc(s_ops, 1)
            groups(pe, NG, 2, 0, body)

        @block.scalar
        def _(act):
            def body(n, u):
                act.wait_ge(s_tps, 2 * n + 1)
                if not under(n, 1):
                    act.wait_ge(s_ops, 2 * n)
                nc.scalar.copy(yT[:, 0, :], bank[0]).then_inc(s_tsb0, 1)
                act.wait_ge(s_osb, 2 * n + 2)
                act.dma_start(outs[bass.ds(n, 1), :, :, :].rearrange("o p t c -> p (o t) c"),
                              xr[:, u, :, :]).then_inc(s_store[u], 16)
            groups(act, NG, 2, 0, body)
            for u in range(2):
                act.wait_ge(s_store[u], 16 * (NG // 2))

        @block.vector
        def _(dve):
            def body(n, u):
                dve.wait_ge(s_tps, 2 * n + 2)
                if not under(n, 1):
                    dve.wait_ge(s_ops, 2 * n)
                nc.vector.tensor_copy(yT[:, 1, :], bank[1]).then_inc(s_tsb1, 1)
                dve.wait_ge(s_load[u], (n - u) * 8 + 16)
                nc.vector.tensor_tensor(xr[:, u, :, :], xr[:, u, :, :], over(core.rows["proj"][:, :], GT, 1),
                                        ALU.add).then_inc(s_xb, 1)
                dve.wait_ge(s_xb, n + 1)
                for h in range(2):
                    dve.wait_ge(s_ops, 2 * n + h + 1)
                    nc.vector.tensor_tensor(xr[:, u, 2 * h:2 * h + 2, :],
                                            bank[2 + h].rearrange("p (t c) -> p t c", t=2),
                                            xr[:, u, 2 * h:2 * h + 2, :], ALU.add).then_inc(s_osb, 1)
            groups(dve, NG, 2, 0, body)



def ffn(core, name, x, y1d, disp, zd, out, base):
    with Phase(core, name) as ph:
        logits = ph.sb("logits", [P, TILES, NE])
        slot = ph.sb("slot", [P, TILES], U32)
        gate = ph.sb("gate", [P, TILES])
        ffn_attention(core, name + "_a", x, y1d, logits)
        route(core, name + "_r", logits, slot, gate)
        dispatch(core, name + "_d", y1d, disp, slot, base)
        experts(core, name + "_e", disp, zd)
        combine(core, name + "_c", x, y1d, zd, out, slot, gate, base)


def macaron(nc, d, out):
    def scratch(name, shape, dt=F32):
        return nc.dram_tensor(name, shape, dt, kind="Internal").ap()

    x = d["L0_attn_x"].rearrange("b t c -> (b t) c")
    y = out.rearrange("b t c -> (b t) c")
    x1, x2, y1d, disp, zd = (scratch(n, (S, C)) for n in ("x1", "x2", "y1d", "disp", "zd"))
    qd, kd = (scratch(n, (B * C, 3, T), BF16) for n in ("qparts", "kparts"))
    relrow = scratch("relrow", (AH, 3 * P))
    neard = scratch("neard", (AH, P, 2 * P))
    with ExitStack() as ctx:
        core = Core(nc, ctx)
        prepare_constants(core, d, relrow, neard)
        prepare_experts(core, d)
        ffn(core, "ffn1", x, y1d, disp, zd, x1, 0)
        with Phase(core, "attention") as ph:
            vall = ph.sb("vall", [P, B * NHG, QB, HG * AD])
            attention_qkv(core, x1, qd, kd, vall)
            attention_core(core, qd, kd, neard, vall)
            attention_out(core, x1, vall, x2)
        ffn(core, "ffn2", x2, y1d, disp, zd, y, 16 * TILES // 4)


_INS = ["L0_attn_x", "L0_attn_W_attn", "L0_attn_b_attn", "L0_attn_W_proj", "L0_attn_b_proj", "L0_attn_rel_emb",
        "L0_ffn_in_proj_w", "L0_ffn_in_proj_b", "L0_ffn_out_proj_w", "L0_ffn_out_proj_b", "L0_ffn_ln1_g",
        "L0_ffn_ln1_b", "L0_ffn_ln2_g", "L0_ffn_ln2_b", "L0_ffn_wg", "L0_ffn_w1", "L0_ffn_b1", "L0_ffn_w2",
        "L0_ffn_b2"]
_OUTS = [((B, T, C), "float32")]


def kernel(**inputs):
    import numpy as _np
    import concourse.bacc as _bacc
    from concourse import mybir as _mybir
    from concourse.bass_utils import run_bass_kernel_spmd as _run

    nc = _bacc.Bacc("TRN2", target_bir_lowering=False, num_devices=1)
    arrays, args = {}, {}
    for name in _INS:
        a = _np.ascontiguousarray(inputs[name])
        arrays[f"in_{name}_dram"] = a
        args[name] = nc.dram_tensor(f"in_{name}_dram", a.shape, _mybir.dt.from_np(a.dtype), kind="ExternalInput").ap()
    (shape, dtype), = _OUTS
    out = nc.dram_tensor("out_0_dram", shape, _mybir.dt.from_np(_np.dtype(dtype)), kind="ExternalOutput").ap()
    macaron(nc, args, out)
    r = _run(nc, [arrays], core_ids=[0])
    return r.results[0]["out_0_dram"]
```

```python
from contextlib import ExitStack

import numpy as np

import concourse.bass as bass
from concourse import mybir

F32 = mybir.dt.float32
BF16 = mybir.dt.bfloat16
I32 = mybir.dt.int32
U32 = mybir.dt.uint32
ALU = mybir.AluOpType
ACT = mybir.ActivationFunctionType
AX = mybir.AxisListType

P = 128
B, T, C = 8, 1024, 256
S = B * T
KB = C // P
TILES = S // P
GT = 4
GW = GT * P
NG = TILES // GT
EPS = 1e-5
FH = 4
FD = C // FH
NE = 8
FF = 1024
CAP = S // NE
AH = 16
AD = C // AH
HG = 4
NHG = AH // HG
QB = T // P
NBUCKET, MAXDIST = 32, 128
BIG = 1e30


def bucket_starts():
    half = NBUCKET // 2
    d = np.arange(2 * P)
    far = half + (np.log(np.maximum(d, half).astype(np.float32) / np.float32(half) + np.float32(1e-10))
                  / np.float32(np.log(MAXDIST / half)) * np.float32(NBUCKET - half)).astype(np.int32)
    bucket = np.where(d < half, d, np.minimum(far, NBUCKET - 1))
    return [int(np.argmax(bucket == b)) if (bucket == b).any() else None for b in range(NBUCKET)]


class Core:

    def __init__(self, nc, ctx):
        self.nc, self.ctx = nc, ctx
        self.ps = ctx.enter_context(nc.psum_tensor("banks", [P, 8, 512], F32))
        self.indirect = [ctx.enter_context(nc.semaphore(f"indirect{i}")) for i in range(8)]

    def keep(self, name, shape, dt=F32):
        return self.ctx.enter_context(self.nc.sbuf_tensor(name, shape, dt))


class Phase(ExitStack):

    def __init__(self, core, name):
        super().__init__()
        self.core, self.name, self.sems = core, name, []

    def sb(self, name, shape, dt=F32):
        return self.enter_context(self.core.nc.sbuf_tensor(f"{self.name}_{name}", shape, dt))

    def sem(self, name):
        sem = self.enter_context(self.core.nc.semaphore(f"{self.name}_{name}"))
        self.sems.append(sem)
        return sem

    def block(self):
        self.callback(self._clear)
        return self.enter_context(self.core.nc.Block())

    def _clear(self):
        for sem in self.sems:
            self.core.nc.gpsimd.sem_clear(sem)
        self.core.nc.all_engine_barrier()


def wait_apart(eng, sem, value):
    eng.wait_ge(sem, value)
    if not isinstance(value, int):
        eng.nop(nofuse=True)


def row_bcast(ap_1d, n):
    return bass.AP(tensor=ap_1d.tensor, offset=ap_1d.offset, ap=[[0, P], [1, n]])


def groups(eng, count, lo, hi, body):
    for g in range(lo):
        body(g, g % 2)
    with eng.Fori(lo // 2, (count - hi) // 2) as it:
        for u in range(2):
            body(it * 2 + u, u)
    for g in range(count - hi, count):
        body(g, g % 2)


def under(g, k):
    return isinstance(g, int) and g < k


def over(ap, count, at):
    return ap.unsqueeze(at).to_broadcast(list(ap.shape[:at]) + [count] + list(ap.shape[at:]))



def prepare_constants(core, d, relrow, neard):
    nc = core.nc
    core.ident = core.keep("ident", [P, P])
    core.identb = core.keep("identb", [P, P], BF16)
    core.mask = core.keep("mask", [P, 4 * P], BF16)
    core.before = core.keep("before", [P, P])
    core.ones = core.keep("ones", [P, P])
    core.winT = core.keep("winT", [P, KB, 3 * C])
    core.woutT = core.keep("woutT", [P, KB, C])
    core.wattnT = core.keep("wattnT", [P, KB, 3 * C])
    core.wprojT = core.keep("wprojT", [P, KB, C])
    core.wg = core.keep("wg", [P, KB, NE])
    core.rows = {k: core.keep("row_" + k, [P, C]) for k in
                 ("ffn_v", "ffn_out", "ln1_g", "ln1_b", "ln2_g", "ln2_b", "attn_v", "proj")}
    core.ffn_qk_b = core.keep("ffn_qk_b", [P, 4])
    core.attn_qk_b = core.keep("attn_qk_b", [P, 4])
    core.mhalf = core.keep("mhalf", [P, GT])
    starts = bucket_starts()
    order = [(b, s) for b, s in enumerate(starts) if s is not None]
    with Phase(core, "const") as ph:
        wraw = ph.sb("wraw", [P, 16, C])
        hankel = ph.sb("hankel", [P, AH, 2 * P])
        toeplitz = ph.sb("toeplitz", [P, AH, 2 * P])
        flip = ph.sb("flip", [P, P])
        embT = ph.sb("embT", [AH, NBUCKET])
        rel = ph.sb("rel", [AH, NBUCKET])
        line = ph.sb("line", [AH, 3 * P])
        zero = ph.sb("zero", [AH, P])
        col = ph.sb("col", [P, P], I32)
        coli = ph.sb("coli", [P, P], I32)
        colf = ph.sb("colf", [P, P])
        s_w, s_emb, s_rows, s_line, s_near, s_neard, s_flip = (
            ph.sem(x) for x in ("w", "emb", "rows", "line", "near", "neard", "flip"))
        s_pool, s_dve, s_ident, s_tps, s_tsb, s_linesb = (
            ph.sem(x) for x in ("pool", "dve", "ident", "tps", "tsb", "linesb"))
        jobs = []
        for m in range(6):
            jobs.append((m, core.winT, m * P))
        for m in range(2):
            jobs.append((6 + m, core.woutT, m * P))
        for m in range(6):
            jobs.append((8 + m, core.wattnT, m * P))
        for m in range(2):
            jobs.append((14 + m, core.wprojT, m * P))

        block = ph.block()

        @block.sync
        def _(sp):
            for k, (name, at, n) in enumerate((("L0_ffn_in_proj_w", 0, 6), ("L0_ffn_out_proj_w", 6, 2),
                                               ("L0_attn_W_attn", 8, 6), ("L0_attn_W_proj", 14, 2))):
                sp.dma_start(wraw[:, at:at + n, :], d[name].rearrange("(m p) c -> p m c", p=P)).then_inc(s_w, 16)
            sp.dma_start(core.wg[:, :, :], d["L0_ffn_wg"].rearrange("(k p) e -> p k e", p=P)).then_inc(s_rows, 16)
            for dst, src, n in (("ffn_v", d["L0_ffn_in_proj_b"][2 * C:3 * C], C), ("ffn_out", d["L0_ffn_out_proj_b"], C),
                                ("ln1_g", d["L0_ffn_ln1_g"], C), ("ln1_b", d["L0_ffn_ln1_b"], C),
                                ("ln2_g", d["L0_ffn_ln2_g"], C), ("ln2_b", d["L0_ffn_ln2_b"], C),
                                ("attn_v", d["L0_attn_b_attn"][2 * C:3 * C], C), ("proj", d["L0_attn_b_proj"], C)):
                sp.dma_start(core.rows[dst][:, :], row_bcast(src, n)).then_inc(s_rows, 16)
            with nc.allow_non_contiguous_dma("small transposed loads"):
                sp.dma_start(embT[:, :], d["L0_attn_rel_emb"].rearrange("b h -> h b")).then_inc(s_emb, 16)
                sp.dma_start(core.ffn_qk_b[:, :], d["L0_ffn_in_proj_b"][0:2 * C].rearrange("(j p) -> p j", p=P)).then_inc(s_emb, 16)
                sp.dma_start(core.attn_qk_b[:, :], d["L0_attn_b_attn"][0:2 * C].rearrange("(j p) -> p j", p=P)).then_inc(s_emb, 16)
            sp.wait_ge(s_linesb, 1)
            sp.dma_start(relrow, line[:, :]).then_inc(s_line, 16)
            sp.wait_ge(s_line, 16)
            for h in range(AH):
                src = bass.AP(tensor=relrow.tensor, offset=h * 3 * P, ap=[[1, P], [1, 2 * P]])
                sp.dma_start(hankel[:, h, :], src).then_inc(s_near, 16)
            sp.wait_ge(s_tsb, len(jobs) + AH // 2)
            sp.dma_start(neard.rearrange("h p k -> p h k"), toeplitz[:, :, :]).then_inc(s_neard, 16)
            sp.wait_ge(s_neard, 16)
            sp.wait_ge(s_rows, 16 * 9)

        @block.gpsimd
        def _(pool):
            nc.gpsimd.memset(core.ident[:, :], 0.0).then_inc(s_pool, 1)
            nc.gpsimd.memset(core.ones[:, :], 1.0).then_inc(s_pool, 1)
            pool.wait_ge(s_pool, 2)
            nc.gpsimd.affine_select(out=core.ident[:, :], in_=core.ident[:, :], compare_op=ALU.not_equal, fill=1.0,
                                    base=0, pattern=[[-1, P]], channel_multiplier=1).then_inc(s_ident, 1)
            nc.gpsimd.affine_select(out=core.before[:, :], in_=core.ones[:, :], compare_op=ALU.is_gt, fill=0.0,
                                    base=0, pattern=[[1, P]], channel_multiplier=-1).then_inc(s_pool, 1)
            nc.gpsimd.iota(col[:, :], pattern=[[1, P]], base=P, channel_multiplier=-1).then_inc(s_ident, 1)
            nc.gpsimd.memset(flip[:, :], 0.0).then_inc(s_pool, 1)
            pool.wait_ge(s_pool, 4)
            nc.gpsimd.affine_select(out=flip[:, :], in_=flip[:, :], compare_op=ALU.not_equal, fill=1.0,
                                    base=1 - P, pattern=[[1, P]], channel_multiplier=1).then_inc(s_flip, 1)
            nc.gpsimd.memset(core.mhalf[:, :], -0.5).then_inc(s_pool, 1)

        @block.vector
        def _(dve):
            n = [0]

            def link(ins):
                n[0] += 1
                ins.then_inc(s_dve, 1)
                dve.wait_ge(s_dve, n[0])

            link(nc.vector.memset(zero[:, :], 0.0))
            dve.wait_ge(s_emb, 48)
            link(nc.vector.tensor_scalar(rel[:, :], embT[:, :], -1.0, embT[:, NBUCKET - 1:NBUCKET], ALU.mult, ALU.add))
            for j, (b, lo) in enumerate(order):
                hi = order[j + 1][1] if j + 1 < len(order) else 2 * P
                w, at = hi - lo, 2 * P - hi
                while w:
                    step = min(w, P)
                    nc.vector.tensor_scalar(line[:, at:at + step], zero[:, 0:step], rel[:, b:b + 1], None, ALU.add)
                    at, w = at + step, w - step
            nc.vector.memset(line[:, 2 * P:3 * P], BIG).then_inc(s_linesb, 1)
            dve.wait_ge(s_ident, 2)
            link(nc.vector.tensor_copy(core.identb[:, :], core.ident[:, :]))
            link(nc.vector.tensor_scalar(coli[:, :], col[:, :], 15, None, ALU.bitwise_and))
            link(nc.vector.tensor_copy(colf[:, :], coli[:, :]))
            for h in range(FH):
                link(nc.vector.tensor_scalar(core.mask[:, h * P:(h + 1) * P], colf[:, :], 1.0, -BIG, ALU.min, ALU.mult))
            dve.wait_ge(s_rows, 16 * 9)
            link(nc.vector.tensor_scalar(core.rows["ln2_g"][:, :], core.rows["ln2_g"][:, :], 0.5, None, ALU.mult))
            link(nc.vector.tensor_scalar(core.rows["ln2_b"][:, :], core.rows["ln2_b"][:, :], 0.5, None, ALU.mult))
            for i, (_, dst, at) in enumerate(jobs):
                dve.wait_ge(s_tps, i + 1)
                nc.vector.tensor_copy(dst[:, :, at:at + P],
                                      core.ps[:, i % 4, 0:KB * P].rearrange("p (k c) -> p k c", k=KB)).then_inc(s_tsb, 1)
            for i in range(len(jobs), len(jobs) + AH // 2):
                dve.wait_ge(s_tps, i + 1)
                h = 2 * (i - len(jobs))
                nc.vector.tensor_copy(toeplitz[:, h:h + 2, :], core.ps[:, i % 4, :].rearrange(
                    "p (h k) -> p h k", h=2)).then_inc(s_tsb, 1)

        @block.tensor
        def _(pe):
            pe.wait_ge(s_ident, 1)
            pe.wait_ge(s_w, 64)
            for i, (slot, _, _) in enumerate(jobs):
                if i >= 4:
                    pe.wait_ge(s_tsb, i - 3)
                for k in range(KB):
                    mm = nc.tensor.transpose(core.ps[:, i % 4, k * P:(k + 1) * P], wraw[:, slot, k * P:(k + 1) * P],
                                             core.ident[:, :])
                mm.then_inc(s_tps, 1)
            pe.wait_ge(s_flip, 1)
            pe.wait_ge(s_near, 16 * AH)
            for i in range(len(jobs), len(jobs) + AH // 2):
                pe.wait_ge(s_tsb, i - 3)
                h = 2 * (i - len(jobs))
                nc.tensor.matmul(core.ps[:, i % 4, :], flip[:, :], hankel[:, h:h + 2, :], start=True,
                                 stop=True).then_inc(s_tps, 1)


def prepare_experts(core, d):
    nc = core.nc
    FB = FF // P
    core.w12 = core.keep("w12", [P, KB, NE * C])
    core.b12 = core.keep("b12", [P, NE * C])
    with Phase(core, "experts") as ph:
        w1 = ph.sb("w1", [P, 2, KB, FF])
        w2 = ph.sb("w2", [P, 2, FB, C])
        w1T = ph.sb("w1T", [P, FB, C])
        b1T = ph.sb("b1T", [P, NE, FB])
        b1w = ph.sb("b1w", [P, FB, P])
        b2r = ph.sb("b2r", [P, NE * C])
        s_w = [ph.sem("w0"), ph.sem("w1")]
        s_b2, s_b1, s_tps, s_tsb, s_w12ps, s_w12sb, s_b1w, s_b12ps, s_b12sb = (
            ph.sem(x) for x in ("b2", "b1", "tps", "tsb", "w12ps", "w12sb", "b1w", "b12ps", "b12sb"))
        block = ph.block()

        @block.sync
        def _(sp):
            sp.dma_start(b2r[:, :], row_bcast(d["L0_ffn_b2"].rearrange("e c -> (e c)"), NE * C)).then_inc(s_b2, 16)

            def body(e, u):
                if not under(e, 2):
                    sp.wait_ge(s_b12ps, e - 1)
                sp.dma_start(w1[:, u, :, :], d["L0_ffn_w1"][bass.ds(e, 1), :, :].rearrange(
                    "o (k p) f -> p (o k) f", p=P)).then_inc(s_w[u], 16)
                sp.dma_start(w2[:, u, :, :], d["L0_ffn_w2"][bass.ds(e, 1), :, :].rearrange(
                    "o (k p) c -> p (o k) c", p=P)).then_inc(s_w[u], 16)
            with nc.allow_non_contiguous_dma("small transposed loads"):
                for e in range(NE):
                    sp.dma_start(b1T[:, e, :], d["L0_ffn_b1"][e, :].rearrange("(k p) -> p k", p=P)).then_inc(s_b1, 16)
            groups(sp, NE, 2, 0, body)

        @block.tensor
        def _(pe):
            def body(e, u):
                half = e // 2 if isinstance(e, int) else None
                pe.wait_ge(s_w[u], (e - u) * 16 + 32)
                for q in range(4):
                    if not under(e, 1):
                        pe.wait_ge(s_tsb, e * 4 - 3 + q)
                    for fb in range(2 * q, 2 * q + 2):
                        for k in range(KB):
                            at = (fb % 2 * KB + k) * P
                            mm = nc.tensor.transpose(core.ps[:, q, at:at + P], w1[:, u, k, fb * P:(fb + 1) * P],
                                                     core.ident[:, :])
                    mm.then_inc(s_tps, 1)
                pe.wait_ge(s_tsb, e * 4 + 4)
                if not under(e, 1):
                    pe.wait_ge(s_w12sb, e)
                for k in range(KB):
                    for fb in range(FB):
                        mm = nc.tensor.matmul(core.ps[:, 4, k * C:(k + 1) * C], w1T[:, fb, k * P:(k + 1) * P],
                                              w2[:, u, fb, :], start=(fb == 0), stop=(fb == FB - 1))
                mm.then_inc(s_w12ps, 1)
                pe.wait_ge(s_b1w, e + 1)
                if not under(e, 1):
                    pe.wait_ge(s_b12sb, e)
                for fb in range(FB):
                    mm = nc.tensor.matmul(core.ps[:, 5, 0:C], b1w[:, fb, :], w2[:, u, fb, :],
                                          start=(fb == 0), stop=(fb == FB - 1))
                mm.then_inc(s_b12ps, 1)
            groups(pe, NE, 2, 0, body)

        def copy_w1T(eng, copy, e, q):
            eng.wait_ge(s_tps, e * 4 + q + 1)
            if not under(e, 1):
                eng.wait_ge(s_w12ps, e)
            copy(w1T[:, 2 * q:2 * q + 2, :], core.ps[:, q, :].rearrange("p (f c) -> p f c", f=2)).then_inc(s_tsb, 1)

        @block.scalar
        def _(act):
            def body(e, u):
                act.wait_ge(s_w12ps, e + 1)
                nc.scalar.copy(core.w12[:, :, bass.ds(e * C, C)],
                               core.ps[:, 4, :].rearrange("p (k c) -> p k c", k=KB)).then_inc(s_w12sb, 1)
            groups(act, NE, 2, 0, body)

        @block.vector
        def _(dve):
            dve.wait_ge(s_b1, 16 * NE)
            dve.wait_ge(s_b2, 16)

            def body(e, u):
                if not under(e, 1):
                    dve.wait_ge(s_b12ps, e)
                nc.vector.tensor_copy(b1w[:, :, :], b1T[:, bass.ds(e, 1), :].rearrange("p o f -> p (o f)")
                                      .unsqueeze(2).to_broadcast([P, FB, P])).then_inc(s_b1w, 1)
                for q in range(4):
                    copy_w1T(dve, nc.vector.tensor_copy, e, q)
                dve.wait_ge(s_b12ps, e + 1)
                nc.vector.tensor_tensor(core.b12[:, bass.ds(e * C, C)], core.ps[:, 5, 0:C], b2r[:, bass.ds(e * C, C)],
                                        ALU.add).then_inc(s_b12sb, 1)
            groups(dve, NE, 2, 0, body)



def ffn_attention(core, name, x, y1d, logits):
    nc = core.nc
    xg = x.rearrange("(p t) c -> p (t c)", p=P)
    y1g = y1d.rearrange("(p t) c -> p (t c)", p=P)
    with Phase(core, name) as ph:
        xin = ph.sb("xin", [P, 2, GT, C])
        xres = ph.sb("xres", [P, 2, GT, C])
        xT = ph.sb("xT", [P, 2, KB, GW])
        qT = ph.sb("qT", [P, 2, 2, GW])
        kT = ph.sb("kT", [P, 2, FH, GW])
        vv = ph.sb("vv", [P, 2, GT, C])
        prob = ph.sb("prob", [P, 2, FH, P])
        probT = ph.sb("probT", [P, FH * P])
        oT = ph.sb("oT", [P, KB, GW])
        res = ph.sb("res", [P, GT, C])
        y1 = ph.sb("y1", [P, 2, GT, C])
        y1T = ph.sb("y1T", [P, KB, GW])
        negm = ph.sb("negm", [P, 2, FH])
        rsum = ph.sb("rsum", [P, 2, FH])
        rinv = ph.sb("rinv", [P, 2, FH])
        xst, xmv, xve, xrs = ph.sb("xst", [P, GT, 6]), ph.sb("xmv", [P, GT, 2]), ph.sb("xve", [P, GT]), ph.sb("xrs", [P, GT])
        yst, ymv, yve, yrs = ph.sb("yst", [P, GT, 6]), ph.sb("ymv", [P, GT, 2]), ph.sb("yve", [P, GT]), ph.sb("yrs", [P, GT])
        s_load = [ph.sem("load0"), ph.sem("load1")]
        s_store = [ph.sem("store0"), ph.sem("store1")]
        (s_xst, s_xmv, s_xve, s_xrs, s_xn, s_xres, s_xTps, s_xTsb, s_qkps, s_qsb, s_ksb, s_vps, s_vsb,
         s_sps, s_negm, s_exp, s_rinv, s_pn, s_pTps, s_pTsb, s_ops, s_osb, s_yps, s_res, s_yst, s_ymv, s_yve, s_yrs,
         s_yn, s_ymul, s_y1, s_yTps, s_yTsb, s_lgps, s_lgsb, s_kz) = (ph.sem(x) for x in (
            "xst", "xmv", "xve", "xrs", "xn", "xres", "xTps", "xTsb", "qkps", "qsb", "ksb", "vps", "vsb",
            "sps", "negm", "exp", "rinv", "pn", "pTps", "pTsb", "ops", "osb", "yps", "res", "yst", "ymv", "yve", "yrs",
            "yn", "ymul", "y1", "yTps", "yTsb", "lgps", "lgsb", "kz"))
        bank = [core.ps[:, i, :] for i in range(8)]
        TR, QK, VY, SC, PT, OO = (0, 1), 2, 3, (4, 5), 6, 7

        def exist(n):
            return not under(n, 1), not isinstance(n, int) or n < NG - 1, not isinstance(n, int) or n < NG - 2

        block = ph.block()

        @block.sync
        def _(sp):
            def store(n, u):
                sp.wait_ge(s_y1, n + 1)
                sp.dma_start(y1g[:, bass.ds(n * GT * C, GT * C)], y1[:, u, :, :].rearrange(
                    "p t c -> p (t c)")).then_inc(s_store[u], 16)

            def body(n, u):
                if not under(n, 2):
                    sp.wait_ge(s_xres, n - 1)
                    sp.wait_ge(s_xTps, 2 * n - 2)
                sp.dma_start(xin[:, u, :, :].rearrange("p t c -> p (t c)"),
                             xg[:, bass.ds(n * GT * C, GT * C)]).then_inc(s_load[u], 16)
                if not under(n, 3):
                    store(n - 3, 1 - u)
            groups(sp, NG, 4, 0, body)
            for n in range(NG - 3, NG):
                store(n, n % 2)
            for u in range(2):
                sp.wait_ge(s_store[u], 16 * (NG // 2))

        @block.tensor
        def _(pe):
            def transpose_x(n, u):
                pe.wait_ge(s_xn, n + 1)
                if not under(n, 3):
                    pe.wait_ge(s_yTsb, 2 * (n - 2))
                elif n:
                    pe.wait_ge(s_xTsb, 2 * n)
                for k in range(KB):
                    for t in range(GT):
                        mm = nc.tensor.transpose(bank[TR[k]][:, t * P:(t + 1) * P], xin[:, u, t, k * P:(k + 1) * P],
                                                 core.ident[:, :])
                    mm.then_inc(s_xTps, 1)

            def project_qk(n, u, j):
                if j == 0:
                    pe.wait_ge(s_xTsb, 2 * n + 2)
                    if not under(n, 3):
                        pe.wait_ge(s_lgsb, n - 2)
                    elif n:
                        pe.wait_ge(s_ksb, 2 * n)
                elif j == 1:
                    pe.wait_ge(s_qsb, 2 * n + 1)
                elif j == 2:
                    pe.wait_ge(s_qsb, 2 * n + 2)
                else:
                    pe.wait_ge(s_ksb, 2 * n + 1)
                for k in range(KB):
                    mm = nc.tensor.matmul(bank[QK], core.winT[:, k, j * P:(j + 1) * P], xT[:, u, k, :],
                                          start=(k == 0), stop=(k == KB - 1))
                mm.then_inc(s_qkps, 1)

            def project_v(n, u, h):
                if h == 0:
                    if not under(n, 2):
                        pe.wait_ge(s_res, 2 * (n - 1))
                    elif n == 1:
                        pe.wait_ge(s_vsb, 2)
                else:
                    if not under(n, 1):
                        pe.wait_ge(s_res, 2 * n - 1)
                    else:
                        pe.wait_ge(s_vsb, 1)
                for t in (2 * h, 2 * h + 1):
                    for k in range(KB):
                        mm = nc.tensor.matmul(bank[VY][:, (t % 2) * C:(t % 2 + 1) * C], xT[:, u, k, t * P:(t + 1) * P],
                                              core.winT[:, k, 2 * C:3 * C], start=(k == 0), stop=(k == KB - 1))
                mm.then_inc(s_vps, 1)

            def scores(n, u, t):
                if t == 0:
                    pe.wait_ge(s_qsb, 2 * n + 2)
                    pe.wait_ge(s_ksb, 2 * n + 2)
                if not (under(n, 1) and t < 2):
                    pe.wait_ge(s_exp, 4 * n + t - 1)
                nc.tensor.matmul(bank[SC[t % 2]], core.identb[:, :], core.mask[:, :], start=True, stop=False,
                                 skip_group_check=True)
                for h in range(FH):
                    mm = nc.tensor.matmul(bank[SC[t % 2]][:, h * P:(h + 1) * P], qT[:, u, h // 2, t * P:(t + 1) * P],
                                          kT[:, u, h, t * P:(t + 1) * P], start=False, stop=(h == FH - 1),
                                          skip_group_check=True)
                mm.then_inc(s_sps, 1)

            def transpose_p(n, t):
                pe.wait_ge(s_pn, 4 * n + t + 1)
                if not (under(n, 1) and t < 1):
                    pe.wait_ge(s_pTsb, 4 * n + t)
                for h in range(FH):
                    mm = nc.tensor.transpose(bank[PT][:, h * P:(h + 1) * P], prob[:, t % 2, h, :], core.ident[:, :])
                mm.then_inc(s_pTps, 1)

            def weigh_v(n, u, t):
                pe.wait_ge(s_pTsb, 4 * n + t + 1)
                pe.wait_ge(s_vsb, 2 * n + t // 2 + 1)
                if not (under(n, 1) and t < 1):
                    pe.wait_ge(s_osb, 4 * n + t)
                for h in range(FH):
                    a = h % 2 * FD
                    mm = nc.tensor.matmul(bank[OO][a:a + FD, (h // 2) * P:(h // 2 + 1) * P],
                                          vv[:, u, t, h * FD:(h + 1) * FD], probT[:, h * P:(h + 1) * P],
                                          start=True, stop=True)
                mm.then_inc(s_ops, 1)

            def project_out(n, h, last):
                pe.wait_ge(s_osb, 4 * n + 2 * h + 2)
                if not last:
                    pe.wait_ge(s_vsb, 2 * n + 3 + h)
                elif h == 0:
                    pe.wait_ge(s_res, 2 * n)
                else:
                    pe.wait_ge(s_res, 2 * n + 1)
                for t in (2 * h, 2 * h + 1):
                    for k in range(KB):
                        mm = nc.tensor.matmul(bank[VY][:, (t % 2) * C:(t % 2 + 1) * C], oT[:, k, t * P:(t + 1) * P],
                                              core.woutT[:, k, :], start=(k == 0), stop=(k == KB - 1))
                mm.then_inc(s_yps, 1)

            def transpose_y(n, u):
                pe.wait_ge(s_y1, n + 1)
                if isinstance(n, int) and n >= NG - 2:
                    pe.wait_ge(s_yTsb, 2 * n)
                else:
                    pe.wait_ge(s_xTsb, 2 * (n + 3))
                for k in range(KB):
                    for t in range(GT):
                        mm = nc.tensor.transpose(bank[TR[k]][:, t * P:(t + 1) * P],
                                                 y1[:, u, t, k * P:(k + 1) * P], core.ident[:, :])
                    mm.then_inc(s_yTps, 1)

            def gate_logits(n):
                pe.wait_ge(s_yTsb, 2 * n + 2)
                if isinstance(n, int) and n >= NG - 2:
                    pe.wait_ge(s_lgsb, n)
                else:
                    pe.wait_ge(s_ksb, 2 * (n + 3))
                for t in range(GT):
                    for k in range(KB):
                        mm = nc.tensor.matmul(bank[QK][:, t * NE:(t + 1) * NE], y1T[:, k, t * P:(t + 1) * P],
                                              core.wg[:, k, :], start=(k == 0), stop=(k == KB - 1))
                mm.then_inc(s_lgps, 1)

            transpose_x(0, 0)
            transpose_x(1, 1)
            for j in range(4):
                project_qk(0, 0, j)
            project_v(0, 0, 0)
            project_v(0, 0, 1)
            pe.wait_ge(s_kz, 1)

            def body(n, u):
                prev, nxt, nxt2 = exist(n)
                scores(n, u, 0)
                scores(n, u, 1)
                if prev:
                    project_out(n - 1, 1, False)
                if nxt:
                    project_qk(n + 1, 1 - u, 0)
                transpose_p(n, 0)
                if nxt:
                    project_qk(n + 1, 1 - u, 1)
                weigh_v(n, u, 0)
                scores(n, u, 2)
                transpose_p(n, 1)
                if nxt:
                    project_qk(n + 1, 1 - u, 2)
                weigh_v(n, u, 1)
                scores(n, u, 3)
                transpose_p(n, 2)
                if nxt:
                    project_qk(n + 1, 1 - u, 3)
                weigh_v(n, u, 2)
                if nxt:
                    project_v(n + 1, 1 - u, 0)
                transpose_p(n, 3)
                if prev:
                    transpose_y(n - 1, 1 - u)
                weigh_v(n, u, 3)
                project_out(n, 0, not nxt)
                if prev:
                    gate_logits(n - 1)
                if nxt:
                    project_v(n + 1, 1 - u, 1)
                if nxt2:
                    transpose_x(n + 2, u)
            groups(pe, NG, 2, 2, body)
            project_out(NG - 1, 1, True)
            transpose_y(NG - 1, (NG - 1) % 2)
            gate_logits(NG - 1)

        @block.scalar
        def _(act):
            def exps(n, t):
                act.wait_ge(s_negm, 4 * n + t + 1)
                for h in range(FH):
                    ins = nc.scalar.activation(prob[:, t % 2, h, :], bank[SC[t % 2]][:, h * P:(h + 1) * P], ACT.Exp,
                                               bias=negm[:, t % 2, h:h + 1], scale=1.0,
                                               accum_out=rsum[:, t % 2, h:h + 1])
                ins.then_inc(s_exp, 1)

            def xT_out(n, u):
                for k in range(KB):
                    act.wait_ge(s_xTps, 2 * n + k + 1)
                    nc.scalar.copy(xT[:, u, k, :], bank[TR[k]]).then_inc(s_xTsb, 1)

            def yT_out(n):
                for k in range(KB):
                    act.wait_ge(s_yTps, 2 * n + k + 1)
                    nc.scalar.copy(y1T[:, k, :], bank[TR[k]]).then_inc(s_yTsb, 1)

            def k_out(n, u, j):
                act.wait_ge(s_qkps, 4 * n + j + 1)
                for a in range(2):
                    r = slice(a * FD, (a + 1) * FD)
                    ins = nc.scalar.activation(kT[r, u, 2 * (j - 2) + a, :], bank[QK][r, :], ACT.Identity,
                                               bias=core.ffn_qk_b[r, j:j + 1], scale=1.0)
                ins.then_inc(s_ksb, 1)

            def o_out(n, t):
                act.wait_ge(s_ops, 4 * n + t + 1)
                nc.scalar.copy(oT[:, :, t * P:(t + 1) * P], bank[OO][:, 0:KB * P].rearrange(
                    "p (k c) -> p k c", k=KB)).then_inc(s_osb, 1)

            act.wait_ge(s_kz, 1)
            xT_out(0, 0)
            xT_out(1, 1)
            k_out(0, 0, 2)
            k_out(0, 0, 3)

            def body(n, u):
                prev, nxt, nxt2 = exist(n)
                exps(n, 0)
                exps(n, 1)
                o_out(n, 0)
                exps(n, 2)
                if nxt:
                    k_out(n + 1, 1 - u, 2)
                o_out(n, 1)
                exps(n, 3)
                if nxt:
                    k_out(n + 1, 1 - u, 3)
                o_out(n, 2)
                if prev:
                    yT_out(n - 1)
                o_out(n, 3)
                if nxt2:
                    xT_out(n + 2, u)
            groups(act, NG, 2, 2, body)
            yT_out(NG - 1)

        @block.vector
        def _(dve):
            def x_stats(n, u):
                dve.wait_ge(s_load[u], (n - u) * 8 + 16)
                for t in range(GT):
                    ins = nc.vector.bn_stats(xst[:, t, :], xin[:, u, t, :])
                ins.then_inc(s_xst, 1)
                wait_apart(dve, s_xst, n + 1)
                for t in range(GT):
                    ins = nc.vector.bn_aggr(xmv[:, t, :], xst[:, t, :])
                ins.then_inc(s_xmv, 1)
                dve.wait_ge(s_xmv, n + 1)
                nc.vector.tensor_scalar(xve[:, :], xmv[:, :, 1], EPS, None, ALU.add).then_inc(s_xve, 1)

            def x_norm(n, u):
                dve.wait_ge(s_xrs, n + 1)
                for t in range(GT):
                    ins = nc.vector.tensor_scalar(xin[:, u, t, :], xin[:, u, t, :], xmv[:, t, 0:1], xrs[:, t:t + 1],
                                                  ALU.subtract, ALU.mult)
                ins.then_inc(s_xn, 1)

            def y_stats(n):
                dve.wait_ge(s_res, 2 * n + 2)
                for t in range(GT):
                    ins = nc.vector.bn_stats(yst[:, t, :], res[:, t, :])
                ins.then_inc(s_yst, 1)
                wait_apart(dve, s_yst, n + 1)
                for t in range(GT):
                    ins = nc.vector.bn_aggr(ymv[:, t, :], yst[:, t, :])
                ins.then_inc(s_ymv, 1)
                dve.wait_ge(s_ymv, n + 1)
                nc.vector.tensor_scalar(yve[:, :], ymv[:, :, 1], EPS, None, ALU.add).then_inc(s_yve, 1)

            def y_norm(n, u):
                dve.wait_ge(s_yrs, n + 1)
                if not under(n, 2):
                    dve.wait_ge(s_store[u], (n - u) * 8)
                    dve.wait_ge(s_yTps, 2 * (n - 1))
                for t in range(GT):
                    ins = nc.vector.tensor_scalar(y1[:, u, t, :], res[:, t, :], ymv[:, t, 0:1], yrs[:, t:t + 1],
                                                  ALU.subtract, ALU.mult)
                ins.then_inc(s_yn, 1)

            def maxima(n, t):
                dve.wait_ge(s_sps, 4 * n + t + 1)
                nc.vector.tensor_reduce(negm[:, t % 2, :], bank[SC[t % 2]].rearrange("p (h c) -> p h c", h=FH),
                                        AX.X, ALU.max, negate=True).then_inc(s_negm, 1)

            def normalise(n, t):
                dve.wait_ge(s_exp, 4 * n + t + 1)
                nc.vector.reciprocal(rinv[:, t % 2, :], rsum[:, t % 2, :]).then_inc(s_rinv, 1)
                dve.wait_ge(s_rinv, 4 * n + t + 1)
                nc.vector.tensor_tensor(prob[:, t % 2, :, :], prob[:, t % 2, :, :], over(rinv[:, t % 2, :], P, 2),
                                        ALU.mult).then_inc(s_pn, 1)

            def pT_out(n, t):
                dve.wait_ge(s_pTps, 4 * n + t + 1)
                nc.vector.tensor_copy(probT[:, :], bank[PT]).then_inc(s_pTsb, 1)

            def q_out(n, u, j):
                dve.wait_ge(s_qkps, 4 * n + j + 1)
                nc.vector.tensor_scalar(qT[:, u, j, :], bank[QK], core.ffn_qk_b[:, j:j + 1], FD ** -0.5,
                                        ALU.add, ALU.mult).then_inc(s_qsb, 1)

            def v_out(n, u, h):
                dve.wait_ge(s_vps, 2 * n + h + 1)
                nc.vector.tensor_tensor(vv[:, u, 2 * h:2 * h + 2, :], bank[VY].rearrange("p (t c) -> p t c", t=2),
                                        over(core.rows["ffn_v"][:, :], 2, 1), ALU.add).then_inc(s_vsb, 1)

            def y_out(n, u, h):
                dve.wait_ge(s_yps, 2 * n + h + 1)
                dve.wait_ge(s_xres, n + 1)
                nc.vector.tensor_tensor(res[:, 2 * h:2 * h + 2, :], bank[VY].rearrange("p (t c) -> p t c", t=2),
                                        xres[:, u, 2 * h:2 * h + 2, :], ALU.add).then_inc(s_res, 1)

            def logits_out(n):
                dve.wait_ge(s_lgps, n + 1)
                nc.vector.tensor_copy(logits[:, bass.ds(n * GT, GT), :], bank[QK][:, 0:GT * NE].rearrange(
                    "p (t e) -> p t e", t=GT)).then_inc(s_lgsb, 1)

            nc.vector.memset(kT[:, :, :, :], 0.0).then_inc(s_kz, 1)
            for n in range(2):
                x_stats(n, n)
                x_norm(n, n)
            q_out(0, 0, 0)
            q_out(0, 0, 1)
            v_out(0, 0, 0)
            v_out(0, 0, 1)

            def body(n, u):
                prev, nxt, nxt2 = exist(n)
                maxima(n, 0)
                maxima(n, 1)
                normalise(n, 0)
                if prev:
                    y_out(n - 1, 1 - u, 1)
                normalise(n, 1)
                if nxt:
                    q_out(n + 1, 1 - u, 0)
                pT_out(n, 0)
                if prev:
                    y_stats(n - 1)
                if nxt:
                    q_out(n + 1, 1 - u, 1)
                maxima(n, 2)
                pT_out(n, 1)
                if prev:
                    y_norm(n - 1, 1 - u)
                normalise(n, 2)
                maxima(n, 3)
                pT_out(n, 2)
                normalise(n, 3)
                if nxt2:
                    x_stats(n + 2, u)
                if nxt:
                    v_out(n + 1, 1 - u, 0)
                pT_out(n, 3)
                y_out(n, u, 0)
                if nxt2:
                    x_norm(n + 2, u)
                if prev:
                    logits_out(n - 1)
                if nxt:
                    v_out(n + 1, 1 - u, 1)
            groups(dve, NG, 2, 2, body)
            y_out(NG - 1, (NG - 1) % 2, 1)
            y_stats(NG - 1)
            y_norm(NG - 1, (NG - 1) % 2)
            logits_out(NG - 1)

        @block.gpsimd
        def _(pool):
            def x_rstd(n):
                pool.wait_ge(s_xve, n + 1)
                nc.gpsimd.tensor_tensor(xrs[:, :], xve[:, :], core.mhalf[:, :], ALU.pow).then_inc(s_xrs, 1)

            def y_rstd(n):
                pool.wait_ge(s_yve, n + 1)
                nc.gpsimd.tensor_tensor(yrs[:, :], yve[:, :], core.mhalf[:, :], ALU.pow).then_inc(s_yrs, 1)

            def y_scale(n, u):
                pool.wait_ge(s_yn, n + 1)
                nc.gpsimd.tensor_tensor(y1[:, u, :, :], y1[:, u, :, :], over(core.rows["ln1_g"][:, :], GT, 1),
                                        ALU.mult).then_inc(s_ymul, 1)

            def y_shift(n, u):
                pool.wait_ge(s_ymul, n + 1)
                nc.gpsimd.tensor_tensor(y1[:, u, :, :], y1[:, u, :, :], over(core.rows["ln1_b"][:, :], GT, 1),
                                        ALU.add).then_inc(s_y1, 1)

            def x_bias(n, u):
                pool.wait_ge(s_xn, n + 1)
                if not under(n, 2):
                    pool.wait_ge(s_res, 2 * (n - 1))
                nc.gpsimd.tensor_tensor(xres[:, u, :, :], xin[:, u, :, :], over(core.rows["ffn_out"][:, :], GT, 1),
                                        ALU.add).then_inc(s_xres, 1)

            x_rstd(0)
            x_rstd(1)
            x_bias(0, 0)

            def body(n, u):
                prev, nxt, nxt2 = exist(n)
                if prev:
                    y_rstd(n - 1)
                    y_scale(n - 1, 1 - u)
                    y_shift(n - 1, 1 - u)
                if nxt2:
                    x_rstd(n + 2)
                if nxt:
                    x_bias(n + 1, 1 - u)
            groups(pool, NG, 2, 2, body)
            y_rstd(NG - 1)
            y_scale(NG - 1, (NG - 1) % 2)
            y_shift(NG - 1, (NG - 1) % 2)



def route(core, name, logits, slot, gate):
    nc = core.nc
    with Phase(core, name) as ph:
        def tile(n, *shape, dt=F32):
            return ph.sb(n, [P, *shape], dt)
        mx, se, first, keep, loc, rank, drop, dscan, t2, t3 = (tile(n, TILES) for n in (
            "mx", "se", "first", "keep", "loc", "rank", "drop", "dscan", "t2", "t3"))
        dif, ex, cand = (tile(n, TILES, NE) for n in ("dif", "ex", "cand"))
        hot, scan, a3, b3 = (tile(n, NE, TILES) for n in ("hot", "scan", "a3", "b3"))
        onest = tile("onest", TILES)
        eidx, ebase, tot, cnt, free, fend, fbeg, off = (tile(n, NE) for n in (
            "eidx", "ebase", "tot", "cnt", "free", "fend", "fbeg", "off"))
        ei = tile("ei", NE, dt=I32)
        rowtot = tile("rowtot", NE + 1)
        base = tile("base", NE + 1)
        s_dve, s_iota, s_dif, s_ex, s_rt, s_base, s_drt, s_dbase = (ph.sem(x) for x in (
            "dve", "iota", "dif", "ex", "rt", "base", "drt", "dbase"))
        bank = [core.ps[:, i, :] for i in range(8)]
        block = ph.block()

        @block.gpsimd
        def _(pool):
            nc.gpsimd.iota(ei[:, :], pattern=[[1, NE]], base=0, channel_multiplier=0).then_inc(s_iota, 1)

        @block.scalar
        def _(act):
            act.wait_ge(s_dif, 1)
            nc.scalar.activation(ex[:, :, :], dif[:, :, :], ACT.Exp).then_inc(s_ex, 1)

        @block.tensor
        def _(pe):
            pe.wait_ge(s_rt, 1)
            nc.tensor.matmul(bank[0][:, 0:NE], core.before[:, :], rowtot[:, 0:NE], start=True, stop=True)
            nc.tensor.matmul(bank[1][:, 0:NE], core.ones[:, :], rowtot[:, 0:NE], start=True, stop=True).then_inc(s_base, 1)
            pe.wait_ge(s_drt, 1)
            nc.tensor.matmul(bank[2][:, 0:1], core.before[:, :], rowtot[:, NE:NE + 1], start=True, stop=True).then_inc(s_dbase, 1)

        @block.vector
        def _(dve):
            n = [0]

            def link(ins):
                n[0] += 1
                ins.then_inc(s_dve, 1)
                dve.wait_ge(s_dve, n[0])

            V = nc.vector
            link(V.tensor_reduce(mx[:, :], logits[:, :, :], AX.X, ALU.max))
            V.tensor_tensor(dif[:, :, :], logits[:, :, :], over(mx[:, :], NE, 2), ALU.subtract).then_inc(s_dif, 1)
            dve.wait_ge(s_iota, 1)
            link(V.tensor_copy(eidx[:, :], ei[:, :]))
            link(V.tensor_scalar(ebase[:, :], eidx[:, :], float(CAP), None, ALU.mult))
            link(V.memset(onest[:, :], 1.0))
            dve.wait_ge(s_dif, 1)
            link(V.tensor_scalar(cand[:, :, :], dif[:, :, :], 0.0, -float(NE), ALU.is_ge, ALU.mult))
            link(V.tensor_tensor(cand[:, :, :], cand[:, :, :], over(eidx[:, :], TILES, 1), ALU.add))
            link(V.tensor_reduce(first[:, :], cand[:, :, :], AX.X, ALU.min))
            link(V.tensor_scalar(first[:, :], first[:, :], float(NE), None, ALU.add))
            link(V.tensor_tensor(hot[:, :, :], over(first[:, :], NE, 1), over(eidx[:, :], TILES, 2), ALU.is_equal))
            for e in range(NE):
                V.tensor_tensor_scan(scan[:, e, :], onest[:, :], hot[:, e, :], 0.0, ALU.mult, ALU.add)
            link(V.memset(t2[:, :], 0.0))
            V.tensor_copy(rowtot[:, 0:NE], scan[:, :, TILES - 1]).then_inc(s_rt, 1)
            dve.wait_ge(s_base, 1)
            link(V.tensor_copy(base[:, 0:NE], bank[0][:, 0:NE]))
            link(V.tensor_copy(tot[:, :], bank[1][:, 0:NE]))
            link(V.tensor_tensor(a3[:, :, :], scan[:, :, :], over(base[:, 0:NE], TILES, 2), ALU.add))
            link(V.tensor_tensor(a3[:, :, :], a3[:, :, :], hot[:, :, :], ALU.mult))
            link(V.tensor_reduce(loc[:, :], a3[:, :, :].rearrange("p e t -> p t e"), AX.X, ALU.add))
            link(V.tensor_scalar(loc[:, :], loc[:, :], -1.0, None, ALU.add))
            link(V.tensor_scalar(keep[:, :], loc[:, :], float(CAP), None, ALU.is_lt))
            link(V.tensor_scalar(drop[:, :], keep[:, :], -1.0, 1.0, ALU.mult, ALU.add))
            link(V.tensor_tensor_scan(dscan[:, :], onest[:, :], drop[:, :], 0.0, ALU.mult, ALU.add))
            V.tensor_copy(rowtot[:, NE:NE + 1], dscan[:, TILES - 1:TILES]).then_inc(s_drt, 1)
            link(V.tensor_scalar(cnt[:, :], tot[:, :], float(CAP), None, ALU.min))
            link(V.tensor_scalar(free[:, :], cnt[:, :], -1.0, float(CAP), ALU.mult, ALU.add))
            link(V.tensor_tensor_scan(fend[:, :], onest[:, 0:NE], free[:, :], 0.0, ALU.mult, ALU.add))
            link(V.tensor_tensor(fbeg[:, :], fend[:, :], free[:, :], ALU.subtract))
            link(V.tensor_tensor(off[:, :], ebase[:, :], cnt[:, :], ALU.add))
            link(V.tensor_tensor(off[:, :], off[:, :], fbeg[:, :], ALU.subtract))
            dve.wait_ge(s_ex, 1)
            link(V.tensor_reduce(se[:, :], ex[:, :, :], AX.X, ALU.add))
            link(V.reciprocal(se[:, :], se[:, :]))
            link(V.tensor_tensor(gate[:, :], se[:, :], keep[:, :], ALU.mult))
            dve.wait_ge(s_dbase, 1)
            link(V.tensor_copy(base[:, NE:NE + 1], bank[2][:, 0:1]))
            link(V.tensor_scalar(rank[:, :], dscan[:, :], base[:, NE:NE + 1], -1.0, ALU.add, ALU.add))
            link(V.tensor_tensor(a3[:, :, :], over(rank[:, :], NE, 1), over(fbeg[:, :], TILES, 2), ALU.is_ge))
            link(V.tensor_tensor(b3[:, :, :], over(rank[:, :], NE, 1), over(fend[:, :], TILES, 2), ALU.is_lt))
            link(V.tensor_tensor(a3[:, :, :], a3[:, :, :], b3[:, :, :], ALU.mult))
            link(V.tensor_tensor(a3[:, :, :], a3[:, :, :], over(off[:, :], TILES, 2), ALU.mult))
            link(V.tensor_reduce(t2[:, :], a3[:, :, :].rearrange("p e t -> p t e"), AX.X, ALU.add))
            link(V.tensor_tensor(t2[:, :], t2[:, :], rank[:, :], ALU.add))
            link(V.tensor_tensor(t2[:, :], t2[:, :], drop[:, :], ALU.mult))
            link(V.scalar_tensor_tensor(out=t3[:, :], in0=first[:, :], scalar=float(CAP), in1=loc[:, :],
                                        op0=ALU.mult, op1=ALU.add))
            link(V.tensor_tensor(t3[:, :], t3[:, :], keep[:, :], ALU.mult))
            link(V.tensor_tensor(t3[:, :], t3[:, :], t2[:, :], ALU.add))
            link(V.tensor_copy(slot[:, :], t3[:, :]))



def dispatch(core, name, y1d, disp, slot, base):
    nc = core.nc
    RING = 4
    y1g = y1d.rearrange("(p t) c -> p (t c)", p=P)
    with Phase(core, name) as ph:
        ring = ph.sb("ring", [P, RING, GT, C])
        s_load = [ph.sem(f"load{i}") for i in range(RING)]
        s_sent = core.indirect[0:RING]
        block = ph.block()

        @block.sync
        def _(sp):
            for n in range(NG):
                if n >= RING:
                    sp.wait_ge(s_sent[n % RING], base + 16 * GT * (n // RING))
                sp.dma_start(ring[:, n % RING, :, :].rearrange("p t c -> p (t c)"),
                             y1g[:, n * GT * C:(n + 1) * GT * C]).then_inc(s_load[n % RING], 16)

        @block.gpsimd
        def _(pool):
            for n in range(NG):
                pool.wait_ge(s_load[n % RING], 16 * (n // RING + 1))
                for t in range(GT):
                    i = n * GT + t
                    pool.indirect_dma_start(disp, bass.IndirectOffsetOnAxis(ap=slot[:, i:i + 1], axis=0),
                                            ring[:, n % RING, t, :], None).then_inc(s_sent[n % RING], 16)
            for r in range(RING):
                pool.wait_ge(s_sent[r], base + 16 * TILES // RING)


def experts(core, name, disp, zd):
    nc = core.nc
    with Phase(core, name) as ph:
        xs = ph.sb("xs", [P, 2, GT, C])
        xT = ph.sb("xT", [P, 2, KB, GW])
        z = ph.sb("z", [P, 2, GT, C])
        s_load = [ph.sem("load0"), ph.sem("load1")]
        s_store = [ph.sem("store0"), ph.sem("store1")]
        s_tps, s_tsb0, s_tsb1, s_zps, s_zsb = (ph.sem(x) for x in ("tps", "tsb0", "tsb1", "zps", "zsb"))
        bank = [core.ps[:, i, :] for i in range(8)]
        rows = disp.rearrange("(g p t) c -> g p (t c)", p=P, t=GT)
        outs = zd.rearrange("(g p t) c -> g p (t c)", p=P, t=GT)
        block = ph.block()

        @block.sync
        def _(sp):
            def body(n, u):
                if not under(n, 2):
                    sp.wait_ge(s_tps, 2 * (n - 1))
                sp.dma_start(xs[:, u, :, :].rearrange("p t c -> p (t c)"), rows[bass.ds(n, 1), :, :].rearrange(
                    "o p c -> p (o c)")).then_inc(s_load[u], 16)
            groups(sp, NG, 2, 0, body)

        @block.tensor
        def _(pe):
            def transposes(n, u):
                pe.wait_ge(s_load[u], (n - u) * 8 + 16)
                if not under(n, 2):
                    pe.wait_ge(s_tsb0, n - 1)
                    pe.wait_ge(s_tsb1, n - 1)
                for k in range(KB):
                    for t in range(GT):
                        mm = nc.tensor.transpose(bank[2 * u + k][:, t * P:(t + 1) * P], xs[:, u, t, k * P:(k + 1) * P],
                                                 core.ident[:, :])
                    mm.then_inc(s_tps, 1)

            def products(n, u):
                pe.wait_ge(s_tsb0, n + 1)
                pe.wait_ge(s_tsb1, n + 1)
                for h in range(2):
                    if not under(n, 1):
                        pe.wait_ge(s_zsb, 2 * n - 1 + h)
                    for t in (2 * h, 2 * h + 1):
                        for k in range(KB):
                            mm = nc.tensor.matmul(bank[4 + h][:, (t % 2) * C:(t % 2 + 1) * C],
                                                  xT[:, u, k, t * P:(t + 1) * P],
                                                  core.w12[:, k, bass.ds((n - u) * (C // 2), C)],
                                                  start=(k == 0), stop=(k == KB - 1))
                    mm.then_inc(s_zps, 1)

            transposes(0, 0)

            def body(n, u):
                if not (isinstance(n, int) and n == NG - 1):
                    transposes(n + 1, 1 - u)
                products(n, u)
            groups(pe, NG, 2, 2, body)

        @block.scalar
        def _(act):
            def xT_out(n, u):
                act.wait_ge(s_tps, 2 * n + 1)
                nc.scalar.copy(xT[:, u, 0, :], bank[2 * u]).then_inc(s_tsb0, 1)

            xT_out(0, 0)

            def body(n, u):
                if not (isinstance(n, int) and n == NG - 1):
                    xT_out(n + 1, 1 - u)
                act.wait_ge(s_zsb, 2 * n + 2)
                act.dma_start(outs[bass.ds(n, 1), :, :].rearrange("o p c -> p (o c)"),
                              z[:, u, :, :].rearrange("p t c -> p (t c)")).then_inc(s_store[u], 16)
            groups(act, NG, 2, 2, body)
            for u in range(2):
                act.wait_ge(s_store[u], 16 * (NG // 2))

        @block.vector
        def _(dve):
            def xT_out(n, u):
                dve.wait_ge(s_tps, 2 * n + 2)
                nc.vector.tensor_copy(xT[:, u, 1, :], bank[2 * u + 1]).then_inc(s_tsb1, 1)

            xT_out(0, 0)

            def body(n, u):
                if not (isinstance(n, int) and n == NG - 1):
                    xT_out(n + 1, 1 - u)
                if not under(n, 2):
                    dve.wait_ge(s_store[u], (n - u) * 8)
                for h in range(2):
                    dve.wait_ge(s_zps, 2 * n + h + 1)
                    nc.vector.tensor_tensor(z[:, u, 2 * h:2 * h + 2, :],
                                            bank[4 + h].rearrange("p (t c) -> p t c", t=2),
                                            over(core.b12[:, bass.ds((n - u) * (C // 2), C)], 2, 1),
                                            ALU.add).then_inc(s_zsb, 1)
            groups(dve, NG, 2, 2, body)


def combine(core, name, x, y1d, zd, out, slot, gate, base):
    nc = core.nc
    RING = 4
    grp = [a.rearrange("(p t) c -> p (t c)", p=P) for a in (x, y1d, out)]
    with Phase(core, name) as ph:
        zr = ph.sb("zr", [P, RING, GT, C])
        y = ph.sb("y", [P, RING, GT, C])
        xr = ph.sb("xr", [P, RING, GT, C])
        res = ph.sb("res", [P, RING, GT, C])
        st = ph.sb("st", [P, GT, 6])
        mv, ve, rs, nb = (ph.sb(n, s) for n, s in (("mv", [P, 2, GT, 2]), ("ve", [P, 2, GT]),
                                                   ("rs", [P, 2, GT]), ("nb", [P, 2, GT])))
        s_got = core.indirect[4:4 + RING]
        s_ld = [ph.sem(f"ld{i}") for i in range(RING)]
        s_out = [ph.sem(f"out{i}") for i in range(RING)]
        s_sum, s_st, s_mv, s_ve, s_sd, s_rs, s_norm, s_inv, s_xb, s_fin = (ph.sem(n) for n in (
            "sum", "st", "mv", "ve", "sd", "rs", "norm", "inv", "xb", "fin"))
        s_scaled = ph.sem("scaled")
        block = ph.block()

        @block.gpsimd
        def _(pool):
            def x_bias(n):
                r = n % RING
                pool.wait_ge(s_ld[r], (n - r) * 8 + 32)
                nc.gpsimd.tensor_tensor(xr[:, r, :, :], xr[:, r, :, :], over(core.rows["ln2_b"][:, :], GT, 1),
                                        ALU.add).then_inc(s_xb, 1)

            for n in range(NG):
                if n >= RING:
                    pool.wait_ge(s_sum, n - RING + 1)
                for t in range(GT):
                    i = n * GT + t
                    pool.indirect_dma_start(zr[:, n % RING, t, :], None, zd,
                                            bass.IndirectOffsetOnAxis(ap=slot[:, i:i + 1], axis=0)
                                            ).then_inc(s_got[n % RING], 16)
                if n >= 2:
                    x_bias(n - 2)
            x_bias(NG - 2)
            x_bias(NG - 1)

        def quads(eng, body):
            for n in range(RING):
                body(n, n)
            with eng.Fori(1, NG // RING - 1) as it:
                for r in range(RING):
                    body(it * RING + r, r)
            for n in range(NG - RING, NG):
                body(n, n % RING)

        @block.sync
        def _(sp):
            def store(n, r):
                sp.wait_ge(s_fin, n + 1)
                sp.dma_start(grp[2][:, bass.ds(n * GT * C, GT * C)], res[:, r, :, :].rearrange(
                    "p t c -> p (t c)")).then_inc(s_out[r], 16)

            def body(n, r):
                if not under(n, RING):
                    sp.wait_ge(s_fin, n - RING + 1)
                for src, dst in ((grp[1], y), (grp[0], xr)):
                    sp.dma_start(dst[:, r, :, :].rearrange("p t c -> p (t c)"),
                                 src[:, bass.ds(n * GT * C, GT * C)]).then_inc(s_ld[r], 16)
                if not under(n, 3):
                    store(n - 3, (r - 3) % RING)
            quads(sp, body)
            for n in range(NG - 3, NG):
                store(n, n % RING)
            for r in range(RING):
                sp.wait_ge(s_out[r], 16 * (NG // RING))

        @block.scalar
        def _(act):
            def root(n, r):
                act.wait_ge(s_ve, n + 1)
                nc.scalar.activation(ve[:, r % 2, :], ve[:, r % 2, :], ACT.Sqrt).then_inc(s_sd, 1)

            root(0, 0)

            def body(n, r):
                if not (isinstance(n, int) and n == NG - 1):
                    root(n + 1, r + 1)
                act.wait_ge(s_rs, n + 1)
                for t in range(GT):
                    ins = nc.scalar.activation(res[:, r, t, :], res[:, r, t, :], ACT.Identity,
                                               bias=nb[:, r % 2, t:t + 1], scale=rs[:, r % 2, t:t + 1])
                ins.then_inc(s_norm, 1)
            quads(act, body)

        @block.vector
        def _(dve):
            def sums(n, r):
                r = r % RING
                dve.wait_ge(s_ld[r], (n - r) * 8 + 32)
                dve.wait_ge(s_got[r], (n - r) * 16 + 16 * GT + base)
                if not under(n, RING):
                    dve.wait_ge(s_out[r], (n - r) * 4)
                for t in range(GT):
                    ins = nc.vector.scalar_tensor_tensor(out=res[:, r, t, :], in0=zr[:, r, t, :],
                                                         scalar=gate[:, bass.ds(n * GT + t, 1)],
                                                         in1=y[:, r, t, :], op0=ALU.mult, op1=ALU.add)
                ins.then_inc(s_sum, 1)
                dve.wait_ge(s_sum, n + 1)
                for t in range(GT):
                    ins = nc.vector.bn_stats(st[:, t, :], res[:, r, t, :])
                ins.then_inc(s_st, 1)
                wait_apart(dve, s_st, n + 1)
                for t in range(GT):
                    ins = nc.vector.bn_aggr(mv[:, r % 2, t, :], st[:, t, :])
                ins.then_inc(s_mv, 1)
                dve.wait_ge(s_mv, n + 1)
                nc.vector.tensor_scalar(ve[:, r % 2, :], mv[:, r % 2, :, 1], EPS, None, ALU.add).then_inc(s_ve, 1)

            def factors(n, r):
                dve.wait_ge(s_sd, n + 1)
                if not under(n, 2):
                    dve.wait_ge(s_norm, n - 1)
                nc.vector.reciprocal(rs[:, r % 2, :], ve[:, r % 2, :]).then_inc(s_inv, 1)
                dve.wait_ge(s_inv, n + 1)
                nc.vector.scalar_tensor_tensor(out=nb[:, r % 2, :], in0=mv[:, r % 2, :, 0], scalar=-1.0,
                                               in1=rs[:, r % 2, :], op0=ALU.mult, op1=ALU.mult).then_inc(s_rs, 1)

            def scale(n, r):
                dve.wait_ge(s_norm, n + 1)
                nc.vector.tensor_tensor(res[:, r % RING, :, :], res[:, r % RING, :, :],
                                        over(core.rows["ln2_g"][:, :], GT, 1), ALU.mult).then_inc(s_scaled, 1)

            def finish(n, r):
                dve.wait_ge(s_scaled, n + 1)
                dve.wait_ge(s_xb, n + 1)
                nc.vector.tensor_tensor(res[:, r % RING, :, :], res[:, r % RING, :, :], xr[:, r % RING, :, :],
                                        ALU.add).then_inc(s_fin, 1)

            sums(0, 0)

            def body(n, r):
                factors(n, r)
                if not (isinstance(n, int) and n == NG - 1):
                    sums(n + 1, r + 1)
                if not under(n, 1):
                    scale(n - 1, r - 1)
                    finish(n - 1, r - 1)
            quads(dve, body)
            scale(NG - 1, NG - 1)
            finish(NG - 1, NG - 1)



def attention_qkv(core, x, qd, kd, vall):
    nc = core.nc
    rows = x.rearrange("(g t p) c -> g p t c", p=P, t=GT)
    with Phase(core, "qkv") as ph:
        xin = ph.sb("xin", [P, 2, GT, C])
        xT = ph.sb("xT", [P, 2, KB, GW])
        f = ph.sb("f", [P, 4, GW])
        part = ph.sb("part", [P, 4, 3, GW], BF16)
        xst, xmv, xve, xrs = ph.sb("xst", [P, GT, 6]), ph.sb("xmv", [P, GT, 2]), ph.sb("xve", [P, GT]), ph.sb("xrs", [P, GT])
        s_load = [ph.sem("load0"), ph.sem("load1")]
        s_store = [ph.sem(f"store{j}") for j in range(4)]
        (s_xst, s_xmv, s_xve, s_xrs, s_xn, s_tps, s_tsb0, s_tsb1, s_qkps, s_f, s_hi, s_r, s_mid, s_lo, s_vps, s_vsb) = (
            ph.sem(x) for x in ("xst", "xmv", "xve", "xrs", "xn", "tps", "tsb0", "tsb1", "qkps", "f", "hi", "r",
                                "mid", "lo", "vps", "vsb"))
        bank = [core.ps[:, i, :] for i in range(8)]
        QK, V = (2, 3, 6, 7), (4, 5)

        def exist(n):
            return not isinstance(n, int) or n < NG - 1, not isinstance(n, int) or n < NG - 2

        block = ph.block()

        @block.sync
        def _(sp):
            def load(n, u):
                if not under(n, 2):
                    sp.wait_ge(s_tps, 2 * (n - 1))
                sp.dma_start(xin[:, u, :, :], rows[bass.ds(n, 1), :, :, :].rearrange(
                    "o p t c -> p (o t) c")).then_inc(s_load[u], 16)

            load(0, 0)
            load(1, 1)

            def body(n, u):
                if exist(n)[1]:
                    load(n + 2, u)
                for j in range(4):
                    sp.wait_ge(s_lo, 4 * n + j + 1)
                    dst = (qd, kd)[j // 2][bass.ds((n - u) * P + (j % 2) * P, P), :, u * GW:(u + 1) * GW]
                    sp.dma_start(dst, part[:, j, :, :]).then_inc(s_store[j], 16)
            groups(sp, NG, 2, 2, body)
            for j in range(4):
                sp.wait_ge(s_store[j], 16 * NG)

        @block.tensor
        def _(pe):
            def transposes(n, u):
                pe.wait_ge(s_xn, n + 1)
                if not under(n, 1):
                    pe.wait_ge(s_tsb0, n)
                    pe.wait_ge(s_tsb1, n)
                for k in range(KB):
                    for t in range(GT):
                        mm = nc.tensor.transpose(bank[k][:, t * P:(t + 1) * P], xin[:, u, t, k * P:(k + 1) * P],
                                                 core.ident[:, :])
                    mm.then_inc(s_tps, 1)

            transposes(0, 0)

            def body(n, u):
                pe.wait_ge(s_tsb0, n + 1)
                pe.wait_ge(s_tsb1, n + 1)
                for j in range(4):
                    if not under(n, 1):
                        pe.wait_ge(s_f, 4 * n + j - 3)
                    for k in range(KB):
                        mm = nc.tensor.matmul(bank[QK[j]], core.wattnT[:, k, j * P:(j + 1) * P], xT[:, u, k, :],
                                              start=(k == 0), stop=(k == KB - 1))
                    mm.then_inc(s_qkps, 1)
                    if j == 1 and exist(n)[0]:
                        transposes(n + 1, 1 - u)
                for h in range(2):
                    if not under(n, 1):
                        pe.wait_ge(s_vsb, 2 * n - 1 + h)
                    for t in (2 * h, 2 * h + 1):
                        for k in range(KB):
                            mm = nc.tensor.matmul(bank[V[h]][:, (t % 2) * C:(t % 2 + 1) * C],
                                                  xT[:, u, k, t * P:(t + 1) * P], core.wattnT[:, k, 2 * C:3 * C],
                                                  start=(k == 0), stop=(k == KB - 1))
                    mm.then_inc(s_vps, 1)
            groups(pe, NG, 2, 2, body)

        @block.scalar
        def _(act):
            def xT_out(n, u):
                act.wait_ge(s_tps, 2 * n + 1)
                nc.scalar.copy(xT[:, u, 0, :], bank[0]).then_inc(s_tsb0, 1)

            def high(n, j):
                act.wait_ge(s_f, 4 * n + j + 1)
                if not under(n, 1):
                    act.wait_ge(s_store[j], 16 * n)
                nc.scalar.copy(part[:, j, 0, :], f[:, j, :]).then_inc(s_hi, 1)

            def middle(n, j):
                act.wait_ge(s_r, 4 * n + j + 1)
                nc.scalar.copy(part[:, j, 1, :], f[:, j, :]).then_inc(s_mid, 1)

            xT_out(0, 0)

            def body(n, u):
                high(n, 0)
                high(n, 1)
                middle(n, 0)
                if exist(n)[0]:
                    xT_out(n + 1, 1 - u)
                high(n, 2)
                middle(n, 1)
                high(n, 3)
                middle(n, 2)
                middle(n, 3)
            groups(act, NG, 2, 2, body)

        @block.vector
        def _(dve):
            def x_stats(n, u):
                dve.wait_ge(s_load[u], (n - u) * 8 + 16)
                for t in range(GT):
                    ins = nc.vector.bn_stats(xst[:, t, :], xin[:, u, t, :])
                ins.then_inc(s_xst, 1)
                wait_apart(dve, s_xst, n + 1)
                for t in range(GT):
                    ins = nc.vector.bn_aggr(xmv[:, t, :], xst[:, t, :])
                ins.then_inc(s_xmv, 1)
                dve.wait_ge(s_xmv, n + 1)
                nc.vector.tensor_scalar(xve[:, :], xmv[:, :, 1], EPS, None, ALU.add).then_inc(s_xve, 1)

            def x_norm(n, u):
                dve.wait_ge(s_xrs, n + 1)
                for t in range(GT):
                    ins = nc.vector.tensor_scalar(xin[:, u, t, :], xin[:, u, t, :], xmv[:, t, 0:1], xrs[:, t:t + 1],
                                                  ALU.subtract, ALU.mult)
                ins.then_inc(s_xn, 1)

            def value(n, j):
                dve.wait_ge(s_qkps, 4 * n + j + 1)
                if not under(n, 1):
                    dve.wait_ge(s_lo, 4 * n + j - 3)
                nc.vector.tensor_scalar(f[:, j, :], bank[QK[j]], core.attn_qk_b[:, j:j + 1],
                                        -(AD ** -0.5) if j < 2 else 1.0, ALU.add, ALU.mult).then_inc(s_f, 1)

            def rest(n, j):
                dve.wait_ge(s_hi, 4 * n + j + 1)
                nc.vector.tensor_tensor(f[:, j, :], f[:, j, :], part[:, j, 0, :], ALU.subtract).then_inc(s_r, 1)

            def xT_out(n, u):
                dve.wait_ge(s_tps, 2 * n + 2)
                nc.vector.tensor_copy(xT[:, u, 1, :], bank[1]).then_inc(s_tsb1, 1)

            def v_out(n, u, h):
                dve.wait_ge(s_vps, 2 * n + h + 1)
                j = u * GT + 2 * h
                nc.vector.tensor_tensor(
                    vall[:, bass.ds((n - u) * 2, NHG), j:j + 2, :].rearrange("p g j d -> p j g d"),
                    bank[V[h]].rearrange("p (t g d) -> p t g d", t=2, g=NHG),
                    over(core.rows["attn_v"].rearrange("p (g d) -> p g d", g=NHG), 2, 1),
                    ALU.add).then_inc(s_vsb, 1)

            x_stats(0, 0)
            x_norm(0, 0)
            xT_out(0, 0)
            x_stats(1, 1)

            def body(n, u):
                nxt, nxt2 = exist(n)
                if nxt:
                    x_norm(n + 1, 1 - u)
                value(n, 0)
                value(n, 1)
                rest(n, 0)
                rest(n, 1)
                value(n, 2)
                if nxt:
                    xT_out(n + 1, 1 - u)
                value(n, 3)
                rest(n, 2)
                rest(n, 3)
                v_out(n, u, 0)
                if nxt2:
                    x_stats(n + 2, u)
                v_out(n, u, 1)
            groups(dve, NG, 2, 2, body)

        @block.gpsimd
        def _(pool):
            def x_rstd(n):
                pool.wait_ge(s_xve, n + 1)
                nc.gpsimd.tensor_tensor(xrs[:, :], xve[:, :], core.mhalf[:, :], ALU.pow).then_inc(s_xrs, 1)

            x_rstd(0)
            x_rstd(1)

            def body(n, u):
                for j in range(4):
                    pool.wait_ge(s_mid, 4 * n + j + 1)
                    nc.gpsimd.tensor_tensor(part[:, j, 2, :], f[:, j, :], part[:, j, 1, :], ALU.subtract).then_inc(s_lo, 1)
                if exist(n)[1]:
                    x_rstd(n + 2)
            groups(pool, NG, 2, 2, body)



Q_PARTS = (0, 0, 0, 1, 1, 2)
K_PARTS = (0, 1, 2, 0, 1, 0)


def attention_core(core, qd, kd, neard, vall):
    nc = core.nc
    NU = B * NHG
    STEPS = QB * HG
    K6 = len(Q_PARTS) * AD

    ORDER = [QB - 1 - m // 2 - m % 2 * (QB // 2) for m in range(QB)]

    def blk(s):
        return ORDER[s // HG]

    def chunks(s):
        n = blk(s) + 1
        return [(0, 0, n - 4), (1, n - 4, 4)] if n > 4 else [(s % 2, 0, n)]

    def done(par, s):
        return sum(c[0] == par for q in range(s + 1) for c in chunks(q))

    PER = done(0, STEPS - 1)
    longest = [max(ORDER[par::2]) + 1 for par in range(2)]
    SLOTS = [sum(longest[q // HG] for q in range(s)) for s in range(2 * HG + 1)]

    with Phase(core, "attn") as ph:
        qst = ph.sb("qst", [K6, 2, HG, T], BF16)
        kst = ph.sb("kst", [K6, 2, HG, T], BF16)
        bias = ph.sb("bias", [P, HG, T])
        vb = ph.sb("vb", [P, 2, QB, HG, 32])
        prob = ph.sb("prob", [P, 2, T])
        probT = ph.sb("probT", [P, SLOTS[-1], P])
        oT = ph.sb("oT", [P, P])
        low = ph.sb("low", [P, 2])
        rsum = ph.sb("rsum", [P, 4, HG])
        rinv = ph.sb("rinv", [P, 2, HG])
        s_load = [ph.sem("load0"), ph.sem("load1")]
        s_near = [ph.sem(f"near{hh}") for hh in range(HG)]
        s_T = [ph.sem("T0"), ph.sem("T1")]
        s_Tsb = [ph.sem("Tsb0"), ph.sem("Tsb1")]
        (s_vz, s_vb, s_S, s_bz, s_low, s_exp, s_O, s_Osb, s_Y, s_rinv, s_y) = (ph.sem(x) for x in (
            "vz", "vb", "S", "bz", "low", "exp", "O", "Osb", "Y", "rinv", "y"))
        LOADS = 16 * 2 * len(Q_PARTS)
        score = [core.ps[:, 0:2, :].rearrange("p a b -> p (a b)"), core.ps[:, 2:4, :].rearrange("p a b -> p (a b)")]
        tbank = [core.ps[:, 4, :], core.ps[:, 5, :]]
        obank = [core.ps[:, 6, 0:P], core.ps[:, 7, 0:P]]
        ybank = [core.ps[:, 6, P:2 * P], core.ps[:, 7, P:2 * P]]

        def probs_of(s, j, w):
            at = SLOTS[s % (2 * HG)] + j
            return probT[:, at:at + w, :]

        def behind(n, u, m):
            return (n, u, m) if m >= 0 else (n - 1, 1 - u, m + QB)

        def ahead(n, u, s):
            return (n, u, s) if s < STEPS else (n + 1, 1 - u, s - STEPS)

        def last(n):
            return isinstance(n, int) and n == NU - 1

        block = ph.block()

        @block.sync
        def _(sp):
            def body(n, u):
                if not under(n, 2):
                    sp.wait_ge(s_S, STEPS * (n - 1))
                for dst, src, parts in ((qst, qd, Q_PARTS), (kst, kd, K_PARTS)):
                    for r, a in enumerate(parts):
                        sp.dma_start(dst[r * AD:(r + 1) * AD, u, :, :],
                                     src[bass.ds(n * HG * AD, HG * AD), a, :].rearrange("(h d) t -> d h t", d=AD)
                                     ).then_inc(s_load[u], 16)
                for hh in range(HG):
                    if not under(n, 1):
                        sp.wait_ge(s_low, STEPS * (n - 1) + STEPS - HG + hh + 1)
                    sp.dma_start(bias[:, hh, T - 2 * P:T], neard[bass.ds(n % NHG * HG + hh, 1), :, :].rearrange(
                        "h p k -> p (h k)")).then_inc(s_near[hh], 16)
            groups(sp, NU, 2, 0, body)

        @block.tensor
        def _(pe):
            def scores(n, u, s):
                n, u, s = ahead(n, u, s)
                i, hh = blk(s), s % HG
                if s == 0:
                    pe.wait_ge(s_load[u], (n - u) * (LOADS // 2) + LOADS)
                if not (under(n, 1) and s < 2):
                    pe.wait_ge(s_exp, STEPS * n + s - 1)
                w = (i + 1) * P
                for a in range(0, w, 512):
                    e = min(w, a + 512)
                    mm = nc.tensor.matmul(score[s % 2][:, a:e], qst[:, u, hh, i * P:(i + 1) * P], kst[:, u, hh, a:e],
                                          start=True, stop=True)
                mm.then_inc(s_S, 1)

            def transposes(n, u, s, part):
                pe.wait_ge(s_exp, STEPS * n + s + 1)
                for par, j0, w in part:
                    before = done(par, s) - 1
                    if not (under(n, 1) and before == 0):
                        pe.wait_ge(s_Tsb[par], PER * n + before)
                    for j in range(w):
                        mm = nc.tensor.transpose(tbank[par][:, j * P:(j + 1) * P],
                                                 prob[:, s % 2, (j0 + j) * P:(j0 + j + 1) * P], core.ident[:, :])
                    mm.then_inc(s_T[par], 1)

            def weigh_v(n, u, m, q):
                n, u, m = behind(n, u, m)
                keys = ORDER[m] + 1
                js = range(keys * q // HG, keys * (q + 1) // HG)
                if not js:
                    return
                if js[0] == 0:
                    if m == 0:
                        pe.wait_ge(s_vb, n + 1)
                    for par in range(2):
                        pe.wait_ge(s_Tsb[par], PER * n + done(par, m * HG + HG - 1))
                    if not (under(n, 1) and m < 2):
                        pe.wait_ge(s_y, QB * n + m - 1)
                for j in js:
                    for hh in range(HG):
                        mm = nc.tensor.matmul(obank[m % 2][32 * hh:32 * hh + 32, :], vb[:, u, j, hh, :],
                                              probs_of(m * HG + hh, j, 1), start=(j == 0),
                                              stop=(j == keys - 1))
                if q == HG - 1:
                    mm.then_inc(s_O, 1)

            def turn_back(n, u, m):
                n, u, m = behind(n, u, m)
                pe.wait_ge(s_Osb, QB * n + m + 1)
                nc.tensor.transpose(ybank[m % 2], oT[:, :], core.ident[:, :]).then_inc(s_Y, 1)

            scores(0, 0, 0)
            scores(0, 0, 1)

            def body(n, u):
                for s in range(STEPS):
                    transposes(n, u, s, chunks(s)[:1])
                    if not (last(n) and s + 2 >= STEPS):
                        scores(n, u, s + 2)
                    transposes(n, u, s, chunks(s)[1:])
                    m = s // HG
                    if not (under(n, 1) and m < 1):
                        weigh_v(n, u, m - 1, s % HG)
                    if s % HG == 2 and not (under(n, 1) and m < 2):
                        turn_back(n, u, m - 2)
            groups(pe, NU, 2, 2, body)
            n, u = NU - 1, (NU - 1) % 2
            turn_back(n, u, QB - 2)
            for q in range(HG):
                weigh_v(n, u, QB - 1, q)
            turn_back(n, u, QB - 1)

        @block.scalar
        def _(act):
            def exps(n, u, s):
                n, u, s = ahead(n, u, s)
                act.wait_ge(s_low, STEPS * n + s + 1)
                for par in range(2):
                    if s >= 2 and done(par, s - 2):
                        act.wait_ge(s_T[par], PER * n + done(par, s - 2))
                    elif not under(n, 1):
                        act.wait_ge(s_T[par], PER * (n - 1) + done(par, STEPS + s - 2))
                m = s // HG
                if s % HG == 0 and not (under(n, 1) and m < 4):
                    act.wait_ge(s_y, QB * n + m - 3)
                w = (blk(s) + 1) * P
                nc.scalar.activation(prob[:, s % 2, 0:w], score[s % 2][:, 0:w], ACT.Exp, bias=low[:, s % 2:s % 2 + 1],
                                     scale=-1.0, accum_out=rsum[:, m % 4, s % HG:s % HG + 1]).then_inc(s_exp, 1)

            def copy_o(n, u, m):
                n, u, m = behind(n, u, m)
                act.wait_ge(s_O, QB * n + m + 1)
                if not (under(n, 1) and m == 0):
                    act.wait_ge(s_Y, QB * n + m)
                nc.scalar.copy(oT[:, :], obank[m % 2]).then_inc(s_Osb, 1)

            exps(0, 0, 0)

            def body(n, u):
                for s in range(STEPS):
                    if not (last(n) and s + 1 >= STEPS):
                        exps(n, u, s + 1)
                    for par, j0, w in chunks(s):
                        if par == 1:
                            act.wait_ge(s_T[1], PER * n + done(1, s))
                            nc.scalar.copy(probs_of(s, j0, w), tbank[1][:, 0:w * P].rearrange(
                                "p (j c) -> p j c", j=w)).then_inc(s_Tsb[1], 1)
                    if s % HG == 1 and not (under(n, 1) and s < 2 * HG):
                        copy_o(n, u, s // HG - 2)
            groups(act, NU, 2, 2, body)
            for m in (QB - 2, QB - 1):
                copy_o(NU - 1, (NU - 1) % 2, m)

        @block.vector
        def _(dve):
            def minimum(n, u, s):
                n, u, s = ahead(n, u, s)
                i, hh = blk(s), s % HG
                if s < HG:
                    dve.wait_ge(s_near[hh], 16 * n + 16)
                wait_apart(dve, s_S, STEPS * n + s + 1)
                w = (i + 1) * P
                part = score[s % 2][:, 0:w]
                nc.vector.tensor_tensor_reduce(out=part, in0=part, in1=bias[:, hh, T - w:T], scale=1.0,
                                               scalar=BIG, op0=ALU.add, op1=ALU.min,
                                               accum_out=low[:, s % 2:s % 2 + 1]).then_inc(s_low, 1)

            def finish(n, u, m):
                n, u, m = behind(n, u, m)
                dve.wait_ge(s_exp, STEPS * n + (m + 1) * HG)
                nc.vector.reciprocal(rinv[:, m % 2, :], rsum[:, m % 4, :]).then_inc(s_rinv, 1)
                dve.wait_ge(s_rinv, QB * n + m + 1)
                dve.wait_ge(s_Y, QB * n + m + 1)
                nc.vector.tensor_tensor(
                    vall[:, bass.ds(n, 1), ORDER[m], :].rearrange("p o (h d) -> p (o h) d", h=HG),
                    ybank[m % 2].rearrange("p (h d) -> p h d", h=HG)[:, :, 0:AD],
                    over(rinv[:, m % 2, :], AD, 2), ALU.mult).then_inc(s_y, 1)

            nc.vector.memset(bias[:, :, 0:T - 2 * P], 0.0).then_inc(s_bz, 1)
            dve.wait_ge(s_bz, 1)
            minimum(0, 0, 0)

            def body(n, u):
                for s in range(STEPS):
                    if not (last(n) and s + 1 >= STEPS):
                        minimum(n, u, s + 1)
                    for par, j0, w in chunks(s):
                        if par == 0:
                            dve.wait_ge(s_T[0], PER * n + done(0, s))
                            nc.vector.tensor_copy(probs_of(s, j0, w), tbank[0][:, 0:w * P].rearrange(
                                "p (j c) -> p j c", j=w)).then_inc(s_Tsb[0], 1)
                    if s % HG == 3 and not (under(n, 1) and s < 2 * HG):
                        finish(n, u, s // HG - 2)
            groups(dve, NU, 2, 2, body)
            for m in (QB - 2, QB - 1):
                finish(NU - 1, (NU - 1) % 2, m)

        @block.gpsimd
        def _(pool):
            nc.gpsimd.memset(vb[:, :, :, :, :], 0.0).then_inc(s_vz, 1)
            pool.wait_ge(s_vz, 1)

            def body(n, u):
                if not under(n, 2):
                    pool.wait_ge(s_O, QB * (n - 1))
                nc.gpsimd.tensor_copy(vb[:, u, :, :, 0:AD], vall[:, bass.ds(n, 1), :, :].rearrange(
                    "p o j (h d) -> p (o j) h d", h=HG)).then_inc(s_vb, 1)
            groups(pool, NU, 2, 0, body)


def attention_out(core, x, vall, out):
    nc = core.nc
    rows, outs = (a.rearrange("(g t p) c -> g p t c", p=P, t=GT) for a in (x, out))
    with Phase(core, "proj") as ph:
        y = ph.sb("y", [P, 2, GT, C])
        yT = ph.sb("yT", [P, 2, KB, GW])
        xr = ph.sb("xr", [P, 2, GT, C])
        s_load = [ph.sem("load0"), ph.sem("load1")]
        s_store = [ph.sem("store0"), ph.sem("store1")]
        s_y, s_xb, s_tps, s_tsb0, s_tsb1, s_ops, s_osb = (ph.sem(x) for x in (
            "y", "xb", "tps", "tsb0", "tsb1", "ops", "osb"))
        bank = [core.ps[:, i, :] for i in range(8)]
        block = ph.block()

        @block.sync
        def _(sp):
            def body(n, u):
                if not under(n, 2):
                    sp.wait_ge(s_store[u], (n - u) * 8)
                sp.dma_start(xr[:, u, :, :], rows[bass.ds(n, 1), :, :, :].rearrange(
                    "o p t c -> p (o t) c")).then_inc(s_load[u], 16)
            groups(sp, NG, 2, 0, body)

        @block.gpsimd
        def _(pool):
            def body(n, u):
                if not under(n, 2):
                    pool.wait_ge(s_tps, 2 * (n - 1))
                nc.gpsimd.tensor_copy(y[:, u, :, :].rearrange("p t (g d) -> p t g d", g=NHG),
                                      vall[:, bass.ds((n - u) * 2, NHG), u * GT:(u + 1) * GT, :].rearrange(
                                          "p g t d -> p t g d")).then_inc(s_y, 1)
            groups(pool, NG, 2, 0, body)

        @block.tensor
        def _(pe):
            def transposes(n, u):
                pe.wait_ge(s_y, n + 1)
                if not under(n, 2):
                    pe.wait_ge(s_tsb0, n - 1)
                    pe.wait_ge(s_tsb1, n - 1)
                for k in range(KB):
                    for t in range(GT):
                        mm = nc.tensor.transpose(bank[2 * u + k][:, t * P:(t + 1) * P], y[:, u, t, k * P:(k + 1) * P],
                                                 core.ident[:, :])
                    mm.then_inc(s_tps, 1)

            transposes(0, 0)

            def body(n, u):
                if not (isinstance(n, int) and n == NG - 1):
                    transposes(n + 1, 1 - u)
                pe.wait_ge(s_tsb0, n + 1)
                pe.wait_ge(s_tsb1, n + 1)
                for h in range(2):
                    if not under(n, 1):
                        pe.wait_ge(s_osb, 2 * n - 1 + h)
                    for t in (2 * h, 2 * h + 1):
                        for k in range(KB):
                            mm = nc.tensor.matmul(bank[4 + h][:, (t % 2) * C:(t % 2 + 1) * C],
                                                  yT[:, u, k, t * P:(t + 1) * P], core.wprojT[:, k, :],
                                                  start=(k == 0), stop=(k == KB - 1))
                    mm.then_inc(s_ops, 1)
            groups(pe, NG, 2, 2, body)

        @block.scalar
        def _(act):
            def yT_out(n, u):
                act.wait_ge(s_tps, 2 * n + 1)
                nc.scalar.copy(yT[:, u, 0, :], bank[2 * u]).then_inc(s_tsb0, 1)

            yT_out(0, 0)

            def body(n, u):
                if not (isinstance(n, int) and n == NG - 1):
                    yT_out(n + 1, 1 - u)
                act.wait_ge(s_osb, 2 * n + 2)
                act.dma_start(outs[bass.ds(n, 1), :, :, :].rearrange("o p t c -> p (o t) c"),
                              xr[:, u, :, :]).then_inc(s_store[u], 16)
            groups(act, NG, 2, 2, body)
            for u in range(2):
                act.wait_ge(s_store[u], 16 * (NG // 2))

        @block.vector
        def _(dve):
            def yT_out(n, u):
                dve.wait_ge(s_tps, 2 * n + 2)
                nc.vector.tensor_copy(yT[:, u, 1, :], bank[2 * u + 1]).then_inc(s_tsb1, 1)

            yT_out(0, 0)

            def body(n, u):
                if not (isinstance(n, int) and n == NG - 1):
                    yT_out(n + 1, 1 - u)
                dve.wait_ge(s_load[u], (n - u) * 8 + 16)
                nc.vector.tensor_tensor(xr[:, u, :, :], xr[:, u, :, :], over(core.rows["proj"][:, :], GT, 1),
                                        ALU.add).then_inc(s_xb, 1)
                dve.wait_ge(s_xb, n + 1)
                for h in range(2):
                    dve.wait_ge(s_ops, 2 * n + h + 1)
                    nc.vector.tensor_tensor(xr[:, u, 2 * h:2 * h + 2, :],
                                            bank[4 + h].rearrange("p (t c) -> p t c", t=2),
                                            xr[:, u, 2 * h:2 * h + 2, :], ALU.add).then_inc(s_osb, 1)
            groups(dve, NG, 2, 2, body)



def ffn(core, name, x, y1d, disp, zd, out, base):
    with Phase(core, name) as ph:
        logits = ph.sb("logits", [P, TILES, NE])
        slot = ph.sb("slot", [P, TILES], U32)
        gate = ph.sb("gate", [P, TILES])
        ffn_attention(core, name + "_a", x, y1d, logits)
        route(core, name + "_r", logits, slot, gate)
        dispatch(core, name + "_d", y1d, disp, slot, base)
        experts(core, name + "_e", disp, zd)
        combine(core, name + "_c", x, y1d, zd, out, slot, gate, base)


def macaron(nc, d, out):
    def scratch(name, shape, dt=F32):
        return nc.dram_tensor(name, shape, dt, kind="Internal").ap()

    x = d["L0_attn_x"].rearrange("b t c -> (b t) c")
    y = out.rearrange("b t c -> (b t) c")
    x1, x2, y1d, disp, zd = (scratch(n, (S, C)) for n in ("x1", "x2", "y1d", "disp", "zd"))
    qd, kd = (scratch(n, (B * C, 3, T), BF16) for n in ("qparts", "kparts"))
    relrow = scratch("relrow", (AH, 3 * P))
    neard = scratch("neard", (AH, P, 2 * P))
    with ExitStack() as ctx:
        core = Core(nc, ctx)
        prepare_constants(core, d, relrow, neard)
        prepare_experts(core, d)
        ffn(core, "ffn1", x, y1d, disp, zd, x1, 0)
        with Phase(core, "attention") as ph:
            vall = ph.sb("vall", [P, B * NHG, QB, HG * AD])
            attention_qkv(core, x1, qd, kd, vall)
            attention_core(core, qd, kd, neard, vall)
            attention_out(core, x1, vall, x2)
        ffn(core, "ffn2", x2, y1d, disp, zd, y, 16 * TILES // 4)


_INS = ["L0_attn_x", "L0_attn_W_attn", "L0_attn_b_attn", "L0_attn_W_proj", "L0_attn_b_proj", "L0_attn_rel_emb",
        "L0_ffn_in_proj_w", "L0_ffn_in_proj_b", "L0_ffn_out_proj_w", "L0_ffn_out_proj_b", "L0_ffn_ln1_g",
        "L0_ffn_ln1_b", "L0_ffn_ln2_g", "L0_ffn_ln2_b", "L0_ffn_wg", "L0_ffn_w1", "L0_ffn_b1", "L0_ffn_w2",
        "L0_ffn_b2"]
_OUTS = [((B, T, C), "float32")]


def kernel(**inputs):
    import numpy as _np
    import concourse.bacc as _bacc
    from concourse import mybir as _mybir
    from concourse.bass_utils import run_bass_kernel_spmd as _run

    nc = _bacc.Bacc("TRN2", target_bir_lowering=False, num_devices=1)
    arrays, args = {}, {}
    for name in _INS:
        a = _np.ascontiguousarray(inputs[name])
        arrays[f"in_{name}_dram"] = a
        args[name] = nc.dram_tensor(f"in_{name}_dram", a.shape, _mybir.dt.from_np(a.dtype), kind="ExternalInput").ap()
    (shape, dtype), = _OUTS
    out = nc.dram_tensor("out_0_dram", shape, _mybir.dt.from_np(_np.dtype(dtype)), kind="ExternalOutput").ap()
    macaron(nc, args, out)
    r = _run(nc, [arrays], core_ids=[0])
    return r.results[0]["out_0_dram"]
```
